# Optimizing a Trainium2 kernel written in Bass

```python
import numpy as np
import jax
import jax.numpy as jnp

def _softmax(x, axis=-1):
    return jax.nn.softmax(x, axis=axis)

def _gelu(x):
    return jax.nn.gelu(x, approximate=True)

def _silu(x):
    return jax.nn.silu(x)

def _sigmoid(x):
    return jax.nn.sigmoid(x)

def _layernorm(x, axis=-1, eps=1e-05):
    m = jnp.mean(x, axis=axis, keepdims=True)
    v = jnp.var(x, axis=axis, keepdims=True)
    return (x - m) / jnp.sqrt(v + eps)

def _scatter_add(tgt, idx, src, axis=0):
    return tgt.at[idx].add(src)

def _segment_sum(src, seg, n):
    return jax.ops.segment_sum(src, seg, n)
kernel_name = 'mk_gps_d1_gnn_r8_bc497d'

def setup_inputs(seed: int=0):
    np.random.seed(seed)
    _w = jnp.asarray

    def _rec_inputs():
        import jax
        import jax.numpy as jnp
        _gk = jax.random.key(seed)
        x = -0.0002117 + 1 * jax.random.normal(jax.random.fold_in(_gk, 1), (6250, 512), jnp.float32)
        src = jax.random.randint(jax.random.fold_in(_gk, 2), (100000,), 0, 6250, jnp.int32)
        dst = jnp.minimum((6250 * jax.random.uniform(jax.random.fold_in(_gk, 3), (100000,)) ** 2.0).astype(jnp.int32), 49999)
        _o = jnp.argsort(dst, stable=True)
        src = src[_o]
        dst = dst[_o]
        return (x, src, dst)
    x, src, dst = _rec_inputs()

    def _L0_gnn_setup():
        import jax, jax.numpy as jnp
        import numpy as np
        N_NODES = 6250
        N_EDGES = 100000
        DIMS = [512, 512, 512, 512]
        NEG_SLOPE = 0.01

        def _mean_agg(h, src, dst):
            s = jax.ops.segment_sum(h[src], dst, num_segments=N_NODES)
            deg = jax.ops.segment_sum(jnp.ones((src.shape[0],), h.dtype), dst, num_segments=N_NODES)
            return s / jnp.maximum(deg, 1.0)[:, None]

        def _sage_layer(h, src, dst, w_self, w_neigh, b):
            h_neigh = _mean_agg(h, src, dst)
            return h @ w_self + h_neigh @ w_neigh + b
        key = jax.random.key(seed)
        ks = jax.random.split(key, 12)
        inp = {'n_feat': jax.random.normal(ks[0], (N_NODES, DIMS[0]), jnp.float32), 'src': jax.random.randint(ks[1], (N_EDGES,), 0, N_NODES, jnp.int32), 'dst': jax.random.randint(ks[2], (N_EDGES,), 0, N_NODES, jnp.int32)}
        for i in range(3):
            din, dout = (DIMS[i], DIMS[i + 1])
            scale = 1.0 / np.sqrt(din)
            inp[f'w_self{i}'] = jax.random.normal(ks[3 + 3 * i], (din, dout), jnp.float32) * scale
            inp[f'w_neigh{i}'] = jax.random.normal(ks[4 + 3 * i], (din, dout), jnp.float32) * scale
            inp[f'b{i}'] = jnp.zeros((dout,), jnp.float32)
        return inp
    _L0_gnn_all = _L0_gnn_setup()
    _L0_gnn_in = {k: v for k, v in _L0_gnn_all.items() if k in ('w_self0', 'w_neigh0', 'b0', 'w_self1', 'w_neigh1', 'b1', 'w_self2', 'w_neigh2', 'b2')}
    del _L0_gnn_all

    def _L0_mix_setup():
        import jax, jax.numpy as jnp
        import numpy as np
        EPS = 1e-06
        key = jax.random.key(seed)
        k1, k2 = jax.random.split(key)
        B, N, C = (8, 512, 512)
        x = jax.random.normal(k1, (B, N, C), dtype=jnp.float32)
        W_qk = jax.random.normal(k2, (2 * C, C), dtype=jnp.float32) * (1.0 / np.sqrt(C))
        return {'x': x, 'W_qk': W_qk}
    _L0_mix_all = _L0_mix_setup()
    _L0_mix_in = {k: v for k, v in _L0_mix_all.items() if k in ('W_qk',)}
    del _L0_mix_all

    def _L0_ffn_setup():
        import jax, jax.numpy as jnp
        import numpy as np
        NUM_EXPERTS = 8
        TOP_K = 2
        HIDDEN = 512
        INTERMEDIATE = 256
        BATCH, SEQ = (8, 256)
        key = jax.random.key(seed)
        ks = jax.random.split(key, 7)
        s_in = 1.0 / np.sqrt(HIDDEN)
        s_mid = 1.0 / np.sqrt(INTERMEDIATE)
        return {'x': jax.random.normal(ks[0], (BATCH, SEQ, HIDDEN), jnp.float32), 'Wg': jax.random.normal(ks[1], (HIDDEN, NUM_EXPERTS), jnp.float32) * s_in, 'bg': jnp.zeros((NUM_EXPERTS,), jnp.float32), 'W1': jax.random.normal(ks[2], (NUM_EXPERTS, HIDDEN, INTERMEDIATE), jnp.float32) * s_in, 'b1': jnp.zeros((NUM_EXPERTS, INTERMEDIATE), jnp.float32), 'W2': jax.random.normal(ks[3], (NUM_EXPERTS, INTERMEDIATE, HIDDEN), jnp.float32) * s_mid, 'b2': jnp.zeros((NUM_EXPERTS, HIDDEN), jnp.float32)}
    _L0_ffn_all = _L0_ffn_setup()
    _L0_ffn_in = {k: v for k, v in _L0_ffn_all.items() if k in ('Wg', 'bg', 'W1', 'b1', 'W2', 'b2')}
    del _L0_ffn_all
    return {'x': x, 'src': src, 'dst': dst, 'L0_gnn_w_self0': _L0_gnn_in['w_self0'], 'L0_gnn_w_neigh0': _L0_gnn_in['w_neigh0'], 'L0_gnn_b0': _L0_gnn_in['b0'], 'L0_gnn_w_self1': _L0_gnn_in['w_self1'], 'L0_gnn_w_neigh1': _L0_gnn_in['w_neigh1'], 'L0_gnn_b1': _L0_gnn_in['b1'], 'L0_gnn_w_self2': _L0_gnn_in['w_self2'], 'L0_gnn_w_neigh2': _L0_gnn_in['w_neigh2'], 'L0_gnn_b2': _L0_gnn_in['b2'], 'L0_mix_W_qk': _L0_mix_in['W_qk'], 'L0_ffn_Wg': _L0_ffn_in['Wg'], 'L0_ffn_bg': _L0_ffn_in['bg'], 'L0_ffn_W1': _L0_ffn_in['W1'], 'L0_ffn_b1': _L0_ffn_in['b1'], 'L0_ffn_W2': _L0_ffn_in['W2'], 'L0_ffn_b2': _L0_ffn_in['b2']}

def reference(x, src, dst, L0_gnn_w_self0, L0_gnn_w_neigh0, L0_gnn_b0, L0_gnn_w_self1, L0_gnn_w_neigh1, L0_gnn_b1, L0_gnn_w_self2, L0_gnn_w_neigh2, L0_gnn_b2, L0_mix_W_qk, L0_ffn_Wg, L0_ffn_bg, L0_ffn_W1, L0_ffn_b1, L0_ffn_W2, L0_ffn_b2):
    import jax
    import jax.numpy as jnp

    def _L0_gnn_ref(n_feat, src, dst, w_self0, w_neigh0, b0, w_self1, w_neigh1, b1, w_self2, w_neigh2, b2):
        import jax, jax.numpy as jnp
        import numpy as np
        N_NODES = 6250
        N_EDGES = 100000
        DIMS = [512, 512, 512, 512]
        NEG_SLOPE = 0.01

        def _mean_agg(h, src, dst):
            s = jax.ops.segment_sum(h[src], dst, num_segments=N_NODES)
            deg = jax.ops.segment_sum(jnp.ones((src.shape[0],), h.dtype), dst, num_segments=N_NODES)
            return s / jnp.maximum(deg, 1.0)[:, None]

        def _sage_layer(h, src, dst, w_self, w_neigh, b):
            h_neigh = _mean_agg(h, src, dst)
            return h @ w_self + h_neigh @ w_neigh + b
        h = n_feat
        h = jax.nn.leaky_relu(_sage_layer(h, src, dst, w_self0, w_neigh0, b0), NEG_SLOPE)
        h = jax.nn.leaky_relu(_sage_layer(h, src, dst, w_self1, w_neigh1, b1), NEG_SLOPE)
        h = jax.nn.leaky_relu(_sage_layer(h, src, dst, w_self2, w_neigh2, b2), NEG_SLOPE)
        return h

    def _L0_mix_ref(x, W_qk):
        import jax, jax.numpy as jnp
        import numpy as np
        EPS = 1e-06
        B, N, C = x.shape
        qk = jnp.einsum('bnc,dc->bnd', x, W_qk).reshape(B, N, 2, C)
        q = jax.nn.elu(qk[:, :, 0]) + 1.0
        k = jax.nn.elu(qk[:, :, 1]) + 1.0
        kv = jnp.einsum('bnd,bne->bde', k, x)
        z = 1.0 / (jnp.einsum('bnd,bd->bn', q, k.sum(axis=1)) + EPS)
        out = jnp.einsum('bnd,bde,bn->bne', q, kv, z)
        return out

    def _L0_ffn_ref(x, Wg, bg, W1, b1, W2, b2):
        import jax, jax.numpy as jnp
        import numpy as np
        NUM_EXPERTS = 8
        TOP_K = 2
        HIDDEN = 512
        INTERMEDIATE = 256
        BATCH, SEQ = (8, 256)
        B, S, H = x.shape
        xf = x.reshape(B * S, H)
        logits = xf @ Wg + bg
        probs = jax.nn.softmax(logits, axis=-1)
        _, top_idx = jax.lax.top_k(probs, TOP_K)
        mask = jnp.any(top_idx[:, :, None] == jnp.arange(NUM_EXPERTS)[None, None, :], axis=1)
        comb = probs * mask.astype(probs.dtype)
        out = jnp.zeros_like(xf)
        for e in range(NUM_EXPERTS):
            h = jax.nn.gelu(xf @ W1[e] + b1[e])
            y = h @ W2[e] + b2[e]
            out = out + comb[:, e:e + 1] * y
        return out.reshape(B, S, H)
    xn = _layernorm(x, axis=-1)
    x = x + _L0_gnn_ref(xn, src, dst, L0_gnn_w_self0, L0_gnn_w_neigh0, L0_gnn_b0, L0_gnn_w_self1, L0_gnn_w_neigh1, L0_gnn_b1, L0_gnn_w_self2, L0_gnn_w_neigh2, L0_gnn_b2) + _L0_mix_ref(xn[None], L0_mix_W_qk)[0]
    x = x + _L0_ffn_ref(_layernorm(x, axis=-1)[None], L0_ffn_Wg, L0_ffn_bg, L0_ffn_W1, L0_ffn_b1, L0_ffn_W2, L0_ffn_b2)[0]
    return x

_drawn_inputs = setup_inputs


def setup_inputs(seed=0):
    import zlib

    import numpy as np

    out = dict(_drawn_inputs(seed))
    spreads = {'L0_gnn_b0': (0.0, 0.1),
     'L0_gnn_b1': (0.0, 0.1),
     'L0_gnn_b2': (0.0, 0.1),
     'L0_ffn_bg': (0.0, 0.1),
     'L0_ffn_b1': (0.0, 0.316),
     'L0_ffn_b2': (0.0, 0.1)}
    factors = {'L0_mix_W_qk': 7.636}
    for name, (base, spread) in spreads.items():
        noise = np.random.default_rng([zlib.crc32(name.encode()), seed]).standard_normal(out[name].shape)
        drawn = base * np.exp(spread * noise) if base else spread * noise
        out[name] = jnp.asarray(drawn.astype(out[name].dtype))
    for name, factor in factors.items():
        out[name] = (out[name] * factor).astype(out[name].dtype)
    return out
```

```python
import concourse.bass as bass
from concourse import mybir
from contextlib import ExitStack

P = 128
C = 512
KB = C // P
N = 6250
NT = -(-N // P)
NPAD = NT * P
E = 100000
GT = 4
RING = 4
NG = -(-E // (P * GT * RING)) * RING
NE = NG * GT
EPAD = NE * P
LAYERS = 3
EXPERTS = 8
F = 256
FB = F // P
LN_EPS = 1e-5
MIX_EPS = 1e-6
SLOPE = 0.01
VL = RING + NG


def build_kernel(nc, x, src, dst, dstg, ws, bs, wqk, wg, bg, w1, b1, w2, b2, out):
    f32, i32, bf16 = mybir.dt.float32, mybir.dt.int32, mybir.dt.bfloat16
    ALU = mybir.AluOpType
    ACT = mybir.ActivationFunctionType
    AX = mybir.AxisListType
    ds = bass.ds

    g_tab = [nc.dram_tensor(f"g_tab{i}", (NPAD, C), f32, kind="Internal").ap() for i in range(2)]
    q_tab = nc.dram_tensor("q_tab", (NT, P, C), f32, kind="Internal").ap()
    xt_tab = nc.dram_tensor("xt_tab", (NT, P, C), f32, kind="Internal").ap()

    x_t = x.rearrange("(t p) f -> t p f", p=P)
    out_t = out.rearrange("(t p) f -> t p f", p=P)

    ctx = ExitStack()
    with ctx:
        def sb(name, shape, dt=f32):
            return ctx.enter_context(nc.sbuf_tensor(name, shape, dt))

        def sem(name):
            return ctx.enter_context(nc.semaphore(name))

        acc = sb("acc", [P, NT, C])
        ident = sb("ident", [P, P])
        ones = sb("ones", [P, 1])
        half = sb("half", [P, NT])
        kv = sb("kv", [P, KB, C])
        ksum = sb("ksum", [P, KB])
        rdeg = sb("rdeg", [P, NT])
        visit = sb("visit", [1, LAYERS * VL], i32)
        window = sb("window", [1, NG], i32)
        mv = sb("mv", [P, NT, 2])
        rstd = sb("rstd", [P, NT])
        logits = sb("logits", [P, NT, EXPERTS])
        comb = sb("comb", [P, NT, EXPERTS])
        wg_sb = sb("wg_sb", [P, KB, EXPERTS])
        bg_sb = sb("bg_sb", [P, EXPERTS])
        ARENA = 23900
        arena = sb("arena", [P, ARENA])
        psum = [ctx.enter_context(nc.psum_tensor(f"psum{i}", [P, C], f32)) for i in range(8)]

        class Plan:
            def __init__(self, at):
                self.at = at

            def take(self, *shape):
                n = 1
                for s in shape:
                    n *= s
                ap = arena[:, self.at:self.at + n]
                self.at += n
                assert self.at <= ARENA, self.at
                if len(shape) == 2:
                    ap = ap.rearrange("p (a b) -> p a b", a=shape[0])
                if len(shape) == 3:
                    ap = ap.rearrange("p (a b c) -> p a b c", a=shape[0], b=shape[1])
                return ap

        edges = Plan(0)
        iota = edges.take(NPAD)
        src_sb = edges.take(NE).bitcast(i32)
        dneg = edges.take(NE)
        AFTER_EDGES = edges.at

        def row_tiles(eng, body):
            body(0, 0, 0)
            body(1, 1, 0)
            with eng.Fori(1, NT // 2) as i:
                body(2 * i, 0, i)
                body(2 * i + 1, 1, i)
            body(NT - 1, 0, NT // 2)

        def need(eng, sem, n):
            if not isinstance(n, int) or n > 0:
                eng.wait_ge(sem, n)

        s_gate = sem("s_gate")

        def gate(eng, sem, n):
            if not isinstance(n, int) or n > 0:
                eng.wait_ge(sem, n)
                eng.sem_inc(s_gate, 1)

        def row(ap, t):
            return ap[:, ds(t, 1), :].rearrange("p a f -> p (a f)")

        def dram_tile(ap, t):
            return ap[ds(t, 1), :, :].rearrange("a p f -> (a p) f")

        def part(ap, k):
            return ap[:, k * P:(k + 1) * P]

        plan = Plan(AFTER_EDGES)
        di = plan.take(NE).bitcast(i32)
        hist = Plan(plan.at)
        dg_i = hist.take(2, C).bitcast(i32)
        dg_f = hist.take(2, C)
        stat = hist.take(2, 6)
        mvt = hist.take(2, 2)
        lohi_f = hist.take(4)
        lohi_i = hist.take(4).bitcast(i32)
        nvis = hist.take(2)
        upto = hist.take(2, VL)
        pick = hist.take(2, NG)
        rowv = hist.take(VL)
        GP = NG // 2
        s_ld, s_x, s_c, s_v, s_st, s_pt, s_pool, s_bn = (sem(n) for n in
            ("s_ld", "s_x", "s_c", "s_v", "s_st", "s_pt", "s_pool", "s_bn"))

        with nc.Block() as block:
            @block.sync
            def _(sp):
                sp.dma_start(src_sb[:, :], src[:, :]).then_inc(s_ld, 16)
                sp.dma_start(di[:, :], dst[:, :]).then_inc(s_ld, 16)
                sp.dma_start(dg_i[0:GP, 0:2, :], dstg[:, :, :]).then_inc(s_ld, 16)
                sp.dma_start(wg_sb[:, :, :], wg.rearrange("(k p) e -> p k e", p=P)).then_inc(s_ld, 16)
                sp.dma_start(bg_sb[:, :], bg.partition_broadcast(P)).then_inc(s_ld, 16)
                sp.wait_ge(s_ld, 80)
                with sp.Fori(0, 7) as i:
                    sp.dma_start(acc[:, ds(i * 7, 7), :],
                                 x_t[ds(i * 7, 7), :, :].rearrange("t p f -> p t f")).then_inc(s_x, 16)

            @block.gpsimd
            def _(pool):
                nc.gpsimd.iota(iota[:, :], pattern=[[1, NPAD]], base=0, channel_multiplier=0,
                               allow_small_or_imprecise_dtypes=True)
                nc.gpsimd.memset(ones[:, :], 1.0)
                nc.gpsimd.memset(half[:, :], -0.5)
                nc.gpsimd.memset(ident[:, :], 0.0).then_inc(s_c, 1)
                nc.gpsimd.memset(upto[:, :, :], 1.0).then_inc(s_c, 1)
                nc.gpsimd.memset(pick[:, :, :], 0.0).then_inc(s_c, 1)
                pool.wait_ge(s_c, 3)
                nc.gpsimd.affine_select(out=ident[:, :], in_=ident[:, :], compare_op=ALU.not_equal, fill=1.0,
                                        base=0, pattern=[[-1, P]], channel_multiplier=1)
                nc.gpsimd.affine_select(out=upto[:, :, :], in_=upto[:, :, :], compare_op=ALU.is_gt, fill=0.0,
                                        base=-(RING - 1), pattern=[[-1, 2], [1, VL]], channel_multiplier=-2)
                nc.gpsimd.affine_select(out=pick[:, :, :], in_=pick[:, :, :], compare_op=ALU.not_equal, fill=1.0,
                                        base=0, pattern=[[1, 2], [-1, NG]],
                                        channel_multiplier=2).then_inc(s_pool, 1)
                pool.wait_ge(s_st, NT + 1)
                nc.gpsimd.tensor_tensor(rstd[:, :], rstd[:, :], half[:, :], ALU.pow).then_inc(s_pool, 1)

            @block.vector
            def _(v):
                v.wait_ge(s_ld, 80)
                nc.vector.tensor_scalar(dneg[:, :], di[:, :], -1.0, None, ALU.mult).then_inc(s_v, 1)
                nc.vector.tensor_copy(dg_f[0:GP, 0:2, :], dg_i[0:GP, 0:2, :]).then_inc(s_v, 1)
                v.wait_ge(s_v, 2)
                nc.vector.tensor_reduce(lohi_f[0:GP, 0:2], dg_f[0:GP, 0:2, :], AX.X, ALU.min)
                nc.vector.tensor_reduce(lohi_f[0:GP, 2:4], dg_f[0:GP, 0:2, :], AX.X, ALU.max).then_inc(s_v, 1)
                v.wait_ge(s_v, 3)
                nc.vector.tensor_copy(lohi_i[0:GP, :], lohi_f[0:GP, :]).then_inc(s_v, 1)
                v.wait_ge(s_v, 4)
                nc.vector.tensor_scalar(lohi_i[0:GP, :], lohi_i[0:GP, :], P.bit_length() - 1, None,
                                        ALU.arith_shift_right).then_inc(s_v, 1)
                v.wait_ge(s_v, 5)
                nc.vector.tensor_copy(lohi_f[0:GP, :], lohi_i[0:GP, :]).then_inc(s_v, 1)
                v.wait_ge(s_v, 6)
                nc.vector.tensor_tensor(nvis[0:GP, :], lohi_f[0:GP, 2:4], lohi_f[0:GP, 0:2],
                                        ALU.subtract).then_inc(s_v, 1)
                v.wait_ge(s_v, 7)
                nc.vector.tensor_scalar(nvis[0:GP, :], nvis[0:GP, :], 1.0, None, ALU.add).then_inc(s_v, 1)
                v.wait_ge(s_pt, 1)
                nc.vector.tensor_copy(rowv[0:1, :], psum[0][0:1, 0:VL]).then_inc(s_v, 1)
                nc.vector.tensor_copy(window[0:1, :], psum[1][0:1, 0:NG])
                v.wait_ge(s_v, 9)
                for l in range(LAYERS):
                    nc.vector.tensor_copy(visit[0:1, l * VL:(l + 1) * VL], rowv[0:1, :]).then_inc(s_v, 1)
                    v.wait_ge(s_v, 10 + 2 * l)
                    nc.vector.tensor_scalar(rowv[0:1, :], rowv[0:1, :], psum[0][0:1, VL - 1:VL], None,
                                            ALU.add).then_inc(s_v, 1)
                    v.wait_ge(s_v, 11 + 2 * l)

                def stats(t, b, k):
                    gate(v, s_st, t - 1)
                    nc.vector.bn_stats(stat[:, b, :], row(acc, t)).then_inc(s_bn, 1)
                    gate(v, s_bn, 2 * t + 1)
                    nc.vector.bn_aggr(mvt[:, b, :], stat[:, b, :]).then_inc(s_bn, 1)
                    v.wait_ge(s_bn, 2 * t + 2)
                    nc.vector.tensor_copy(row(mv, t), mvt[:, b, :]).then_inc(s_st, 1)
                v.wait_ge(s_x, 16 * 7)
                row_tiles(v, stats)
                v.wait_ge(s_st, NT)
                nc.vector.tensor_scalar(rstd[:, :], mv[:, :, 1], LN_EPS, None, ALU.add).then_inc(s_st, 1)
                v.wait_ge(s_pool, 2)

            @block.tensor
            def _(pe):
                pe.wait_ge(s_v, 8)
                pe.wait_ge(s_pool, 1)
                for j in range(2):
                    nc.tensor.matmul(psum[0][0:1, 0:VL], nvis[0:GP, j:j + 1], upto[0:GP, j, :],
                                     start=(j == 0), stop=(j == 1))
                for j in range(2):
                    last = nc.tensor.matmul(psum[1][0:1, 0:NG], lohi_f[0:GP, j:j + 1], pick[0:GP, j, :],
                                            start=(j == 0), stop=(j == 1))
                last.then_inc(s_pt, 1)

        plan = Plan(AFTER_EDGES)
        di = plan.take(NE).bitcast(i32)
        dr_i = plan.take(NE).bitcast(i32)
        dw_i = plan.take(NE).bitcast(i32)
        dr = plan.take(NE)
        dw = plan.take(NE)
        hot_r = [plan.take(GT * P // 2).bitcast(bf16).rearrange("p (j r) -> p j r", j=GT) for _ in range(2)]
        hot_w = [plan.take(GT * 50 // 2).bitcast(bf16).rearrange("p (j r) -> p j r", j=GT) for _ in range(2)]
        deg = psum[2][:, 0:NT]
        s_dv, s_hot, s_deg = (sem(n) for n in ("s_dv", "s_hot", "s_deg"))

        with nc.Block() as block:
            @block.vector
            def _(v):
                nc.vector.tensor_scalar(dr_i[:, :], di[:, :], P - 1, None, ALU.bitwise_and).then_inc(s_dv, 1)
                nc.vector.tensor_scalar(dw_i[:, :], di[:, :], P.bit_length() - 1, None,
                                        ALU.arith_shift_right).then_inc(s_dv, 1)
                v.wait_ge(s_dv, 2)
                nc.vector.tensor_copy(dr[:, :], dr_i[:, :]).then_inc(s_dv, 1)
                nc.vector.tensor_copy(dw[:, :], dw_i[:, :]).then_inc(s_dv, 1)
                v.wait_ge(s_dv, 4)

                def hots(g, b):
                    need(v, s_deg, g - 1)
                    nc.vector.tensor_tensor(hot_r[b][:, :, :],
                                            iota[:, 0:P].unsqueeze(1).to_broadcast([P, GT, P]),
                                            dr[:, ds(g * GT, GT)].unsqueeze(2).to_broadcast([P, GT, P]),
                                            ALU.is_equal)
                    nc.vector.tensor_tensor(hot_w[b][:, :, 0:NT],
                                            iota[:, 0:NT].unsqueeze(1).to_broadcast([P, GT, NT]),
                                            dw[:, ds(g * GT, GT)].unsqueeze(2).to_broadcast([P, GT, NT]),
                                            ALU.is_equal).then_inc(s_hot, 1)
                hots(0, 0)
                hots(1, 1)
                with v.Fori(1, NG // 2) as i:
                    hots(2 * i, 0)
                    hots(2 * i + 1, 1)
                v.wait_ge(s_deg, NG)
                nc.vector.tensor_scalar(rdeg[:, :], deg, 1.0, None, ALU.max).then_inc(s_dv, 1)
                v.wait_ge(s_dv, 5)
                nc.vector.reciprocal(rdeg[:, :], rdeg[:, :]).then_inc(s_dv, 1)

            @block.tensor
            def _(pe):
                def count(g, b, first=False, final=False):
                    pe.wait_ge(s_hot, g + 1)
                    for j in range(GT):
                        last = nc.tensor.matmul(deg, hot_r[b][:, j, :], hot_w[b][:, j, 0:NT],
                                                start=first and j == 0, stop=final and j == GT - 1)
                    last.then_inc(s_deg, 1)
                count(0, 0, first=True)
                count(1, 1)
                with pe.Fori(1, NG // 2 - 1) as i:
                    count(2 * i, 0)
                    count(2 * i + 1, 1)
                count(NG - 2, 0)
                count(NG - 1, 1, final=True)

        WAT = 19200
        plan = Plan(WAT)
        wn_sb = plan.take(KB, C)
        ws_sb = plan.take(KB, C)
        bias = plan.take(C)
        plan = Plan(AFTER_EDGES)
        wqk_sb = plan.take(KB, 2 * C)
        xn = [plan.take(C) for _ in range(2)]
        xT = [plan.take(C) for _ in range(2)]
        gbuf = [plan.take(C) for _ in range(2)]
        kbuf = [plan.take(C) for _ in range(2)]
        qbuf = [plan.take(C) for _ in range(2)]
        ek, eq = plan.take(C), plan.take(C)
        kacc = plan.take(C)
        assert plan.at <= WAT
        tT, tK, tG, tS, tQ = psum[4], psum[5], psum[6], psum[7], psum[5]
        s_w = sem("s_w")
        (s_xn, s_k, s_xT, s_s, s_q, s_ek, s_g, s_eq, s_pk, s_pg, s_pT, s_ps, s_pq, s_pkv, s_kacc, s_m) = (
            sem("c_" + n) for n in "xn k xT s q ek g eq pk pg pT ps pq pkv kacc m".split())
        s_gst = [sem(f"c_gst{b}") for b in range(2)]
        s_qst = [sem(f"c_qst{b}") for b in range(2)]
        LAST = NT - 1

        with nc.Block() as block:
            @block.sync
            def _(sp):
                sp.dma_start(wn_sb[:, :, :], ws[1, 0].rearrange("(k p) f -> p k f", p=P)).then_inc(s_w, 16)
                sp.dma_start(ws_sb[:, :, :], ws[0, 0].rearrange("(k p) f -> p k f", p=P)).then_inc(s_w, 16)
                sp.dma_start(wqk_sb[:, :, :], wqk.rearrange("(k p) f -> p k f", p=P)).then_inc(s_w, 16)
                sp.dma_start(bias[:, :], bs[0].partition_broadcast(P)).then_inc(s_w, 16)

                def store(t, b, k):
                    sp.wait_ge(s_g, t + 1)
                    sp.dma_start(g_tab[0][ds(t * P, P), :], gbuf[b][:, :]).then_inc(s_gst[b], 16)
                    sp.wait_ge(s_q, t + 1)
                    sp.dma_start(dram_tile(q_tab, t), qbuf[b][:, :]).then_inc(s_qst[b], 16)
                row_tiles(sp, store)
                for b in range(2):
                    turns = NT // 2 + (1 - b) * (NT % 2)
                    sp.wait_ge(s_gst[b], 16 * turns)
                    sp.wait_ge(s_qst[b], 16 * turns)

            @block.gpsimd
            def _(pool):
                nc.gpsimd.memset(kacc[:, :], 0.0).then_inc(s_kacc, 1)

                def add_keys(t, b, k):
                    pool.wait_ge(s_k, t + 1)
                    pool.wait_ge(s_kacc, t + 1)
                    rows = N - LAST * P if isinstance(t, int) and t == LAST else P
                    nc.gpsimd.tensor_tensor(kacc[0:rows, :], kacc[0:rows, :], kbuf[b][0:rows, :],
                                            ALU.add).then_inc(s_kacc, 1)
                row_tiles(pool, add_keys)

            @block.scalar
            def _(act):
                def exp_negative(e, product, m, done):
                    nc.scalar.activation(e[:, :], product[:, :], ACT.Relu, scale=-1.0).then_inc(s_m, 1)
                    act.wait_ge(s_m, m)
                    nc.scalar.activation(e[:, :], e[:, :], ACT.Exp, scale=-1.0).then_inc(done, 1)

                def body(t, b, k):
                    act.wait_ge(s_pk, t + 1)
                    need(act, s_k, t)
                    exp_negative(ek, tK, 2 * t + 1, s_ek)
                    act.wait_ge(s_pg, t + 1)
                    need(act, s_gst[b], 16 * k)
                    nc.scalar.copy(gbuf[b][:, :], tG[:, :]).then_inc(s_g, 1)
                    act.wait_ge(s_pq, t + 1)
                    need(act, s_q, t)
                    exp_negative(eq, tQ, 2 * t + 2, s_eq)
                row_tiles(act, body)

            @block.vector
            def _(v):
                def normalise(t, b):
                    need(v, s_pkv, t - 1)
                    nc.vector.tensor_scalar(xn[b][:, :], row(acc, t), row(mv, t)[:, 0:1],
                                            rstd[:, ds(t, 1)], ALU.subtract, ALU.mult).then_inc(s_xn, 1)

                def keep_transposed(t, b):
                    v.wait_ge(s_pT, t + 1)
                    need(v, s_pq, t - 1)
                    nc.vector.tensor_copy(xT[b][:, :], tT[:, :]).then_inc(s_xT, 1)

                def feature(e, product, to, done):
                    nc.vector.scalar_tensor_tensor(to, product[:, :], 0.0, e[:, :], ALU.max,
                                                   ALU.add).then_inc(done, 1)

                normalise(0, 0)
                keep_transposed(0, 0)
                v.wait_ge(s_w, 64)

                def body(t, b, k):
                    more = not (isinstance(t, int) and t == LAST)
                    if more:
                        normalise(t + 1, 1 - b)
                    v.wait_ge(s_ek, t + 1)
                    need(v, s_kacc, t)
                    need(v, s_pkv, t - 1)
                    feature(ek, tK, kbuf[b][:, :], s_k)
                    if more:
                        keep_transposed(t + 1, 1 - b)
                    v.wait_ge(s_ps, t + 1)
                    nc.vector.tensor_tensor(row(acc, t), tS[:, :], bias[:, :], ALU.add).then_inc(s_s, 1)
                    v.wait_ge(s_eq, t + 1)
                    need(v, s_qst[b], 16 * k)
                    feature(eq, tQ, qbuf[b][:, :], s_q)
                row_tiles(v, body)
                v.wait_ge(s_pkv, NT + 1)
                for d in range(KB):
                    nc.vector.tensor_copy(kv[:, d, :], psum[d][:, :])
                nc.vector.tensor_copy(ksum[:, :], psum[4][:, 0:KB])

            @block.tensor
            def _(pe):
                def turn(t, b):
                    pe.wait_ge(s_xn, t + 1)
                    need(pe, s_xT, t)
                    for c in range(KB):
                        last = nc.tensor.transpose(part(tT, c), part(xn[b], c), ident[:, :])
                    last.then_inc(s_pT, 1)

                turn(0, 0)
                pe.wait_ge(s_w, 64)

                def body(t, b, k):
                    more = not (isinstance(t, int) and t == LAST)
                    pe.wait_ge(s_xT, t + 1)
                    need(pe, s_q, t)
                    for c in range(KB):
                        last = nc.tensor.matmul(tK[:, :], part(xT[b], c), wqk_sb[:, c, C:2 * C],
                                                start=(c == 0), stop=(c == KB - 1))
                    last.then_inc(s_pk, 1)
                    need(pe, s_g, t)
                    for c in range(KB):
                        last = nc.tensor.matmul(tG[:, :], part(xT[b], c), wn_sb[:, c, :],
                                                start=(c == 0), stop=(c == KB - 1))
                    last.then_inc(s_pg, 1)
                    if more:
                        turn(t + 1, 1 - b)
                    need(pe, s_s, t)
                    for c in range(KB):
                        last = nc.tensor.matmul(tS[:, :], part(xT[b], c), ws_sb[:, c, :],
                                                start=(c == 0), stop=(c == KB - 1))
                    last.then_inc(s_ps, 1)
                    pe.wait_ge(s_k, t + 1)
                    for d in range(KB):
                        for c in range(KB):
                            last = nc.tensor.matmul(part(tQ, d), wqk_sb[:, c, d * P:(d + 1) * P], part(xT[b], c),
                                                    start=(c == 0), stop=(c == KB - 1))
                    last.then_inc(s_pq, 1)
                    first = isinstance(t, int) and t == 0
                    for d in range(KB):
                        last = nc.tensor.matmul(psum[d][:, :], part(kbuf[b], d), xn[b][:, :],
                                                start=first, stop=not more)
                    last.then_inc(s_pkv, 1)
                row_tiles(pe, body)
                pe.wait_ge(s_kacc, NT + 1)
                for d in range(KB):
                    last = nc.tensor.matmul(psum[4][:, d:d + 1], part(kacc, d), ones[:, :], start=True, stop=True)
                last.then_inc(s_pkv, 1)

        plan = Plan(AFTER_EDGES)
        rows = [plan.take(GT, C) for _ in range(RING)]
        hot = [plan.take(GT, P) for _ in range(RING)]
        dist = [plan.take(GT, P) for _ in range(2)]
        idx = [plan.take(GT).bitcast(i32) for _ in range(RING)]
        assert plan.at <= WAT
        s_rows = [sem(f"a_rows{b}") for b in range(RING)]
        s_idx, s_dist, s_hot2, s_used, s_acc = (sem("a_" + n) for n in "idx dist hot used acc".split())

        def aggregate(l):
            tab = g_tab[l % 2]

            def entry(eng, k):
                return eng.value_load(visit[0:1, ds(k + l * VL, 1)], min_val=0, max_val=LAYERS * NG * NT)

            def groups(eng, body):
                with eng.Fori(0, NG // RING) as it:
                    for b in range(RING):
                        body(RING * it + b, b, it)

            def window_of(n, v0, w0):
                return w0 if n is v0 else nc.s_assert_within(
                    n - v0 + w0, 0, NT - 1, skip_runtime_bounds_check_because="a group has a visit per window")

            def bounds(eng, g):
                return entry(eng, g + RING - 1), entry(eng, g + RING)

            def visits(eng, v0, v1, first_of, other):
                first_of(v0)
                with eng.If(v0 + 1 < v1):
                    with eng.Fori(v0 + 1, v1) as n:
                        other(n, v0)

            with nc.Block() as block:
                @block.sync
                def _(sp):
                    if l + 1 < LAYERS:
                        sp.dma_start(wn_sb[:, :, :], ws[1, l + 1].rearrange("(k p) f -> p k f", p=P)).then_inc(s_w, 16)
                        sp.dma_start(ws_sb[:, :, :], ws[0, l + 1].rearrange("(k p) f -> p k f", p=P)).then_inc(s_w, 16)
                        sp.dma_start(bias[:, :], bs[l + 1].partition_broadcast(P)).then_inc(s_w, 16)
                        sp.wait_ge(s_w, 64 + 48 * (l + 1))

                @block.gpsimd
                def _(pool):
                    def body(g, b, it):
                        gate(pool, s_idx, g + (l * NG + 1))
                        for j in range(GT):
                            nc.gpsimd.indirect_dma_start(
                                out=rows[b][:, j, :], out_offset=None, in_=tab[:, :],
                                in_offset=bass.IndirectOffsetOnAxis(ap=idx[b][:, j:j + 1], axis=0),
                            ).then_inc(s_rows[b], 16)
                    groups(pool, body)

                @block.scalar
                def _(act):
                    if l == 0:
                        act.sem_inc(s_used, 1)
                        act.sem_inc(s_acc, 1)

                    def matrices(g, b, n, v0, w0):
                        w = window_of(n, v0, w0)
                        nodes = iota[:, ds(w * P, P)]
                        for j in range(GT):
                            last = nc.scalar.activation(dist[b % 2][:, j, :], nodes, ACT.Abs,
                                                        bias=dneg[:, ds(g * GT + j, 1)])
                        last.then_inc(s_dist, 1)
                        act.wait_ge(s_dist, n + 1)
                        nc.scalar.activation(hot[b][:, :, :], dist[b % 2][:, :, :], ACT.Relu, bias=1.0,
                                             scale=-1.0).then_inc(s_hot2, 1)

                    def body(g, b, it):
                        free = entry(act, g)
                        act.wait_ge(s_used, free + 1)
                        nc.scalar.copy(idx[b][:, :], src_sb[:, ds(g * GT, GT)]).then_inc(s_idx, 1)
                        w0 = act.value_load(window[0:1, ds(g, 1)], min_val=0, max_val=NT - 1)

                        def rest(n, v0):
                            act.wait_ge(s_used, n + 1)
                            matrices(g, b, n, v0, w0)
                        visits(act, *bounds(act, g), lambda v0: matrices(g, b, v0, v0, w0), rest)
                    groups(act, body)

                @block.tensor
                def _(pe):
                    def products(b, n):
                        pe.wait_ge(s_hot2, n + 1)
                        for j in range(GT):
                            last = nc.tensor.matmul(psum[b][:, :], hot[b][:, j, :], rows[b][:, j, :],
                                                    start=(j == 0), stop=(j == GT - 1))
                        last.then_inc(s_used, 1)

                    def body(g, b, it):
                        free = entry(pe, g)
                        v0, v1 = bounds(pe, g)
                        pe.wait_ge(s_rows[b], (it + (l * (NG // RING) + 1)) * (16 * GT))
                        pe.wait_ge(s_acc, free + 1)

                        def rest(n, v0):
                            pe.wait_ge(s_acc, n + 1)
                            products(b, n)
                        visits(pe, v0, v1, lambda v0: products(b, v0), rest)
                    groups(pe, body)

                @block.vector
                def _(v):
                    def add(g, b, n, v0, w0):
                        w = window_of(n, v0, w0)
                        v.wait_ge(s_used, n + 2)
                        v.wait_ge(s_acc, n + 1)
                        nc.vector.scalar_tensor_tensor(row(acc, w), psum[b][:, :], rdeg[:, ds(w, 1)],
                                                       row(acc, w), ALU.mult, ALU.add).then_inc(s_acc, 1)

                    def body(g, b, it):
                        w0 = v.value_load(window[0:1, ds(g, 1)], min_val=0, max_val=NT - 1)
                        visits(v, *bounds(v, g), lambda v0: add(g, b, v0, v0, w0), lambda n, v0: add(g, b, n, v0, w0))
                    groups(v, body)

        plan = Plan(AFTER_EDGES)
        h = [plan.take(C) for _ in range(2)]
        hT = [plan.take(C) for _ in range(2)]
        gout = [plan.take(C) for _ in range(2)]
        e_h, e_hT, e_s, e_g, e_pT, e_pg, e_ps = (sem("e_" + n) for n in "h hT s g pT pg ps".split())
        e_gst = [sem(f"e_gst{b}") for b in range(2)]

        def dense(l):
            o = (l - 1) * NT
            with nc.Block() as block:
                @block.sync
                def _(sp):
                    def store(t, b, k):
                        sp.wait_ge(e_g, t + (o + 1))
                        sp.dma_start(g_tab[l % 2][ds(t * P, P), :], gout[b][:, :]).then_inc(e_gst[b], 16)
                    row_tiles(sp, store)
                    for b in range(2):
                        sp.wait_ge(e_gst[b], 16 * l * (NT // 2 + (1 - b) * (NT % 2)))

                @block.scalar
                def _(act):
                    def body(t, b, k):
                        act.wait_ge(e_pg, t + (o + 1))
                        need(act, e_gst[b], k * 16 + 16 * (l - 1) * (NT // 2 + (1 - b) * (NT % 2)))
                        nc.scalar.copy(gout[b][:, :], psum[2 + b][:, :]).then_inc(e_g, 1)
                    row_tiles(act, body)

                @block.vector
                def _(v):
                    def leaky(t, b):
                        need(v, e_pT, t + (o - 1))
                        nc.vector.scalar_tensor_tensor(h[b][:, :], row(acc, t), SLOPE, row(acc, t),
                                                       ALU.mult, ALU.max).then_inc(e_h, 1)

                    def keep_transposed(t, b):
                        v.wait_ge(e_pT, t + (o + 1))
                        need(v, e_ps, t + (o - 1))
                        nc.vector.tensor_copy(hT[b][:, :], psum[b][:, :]).then_inc(e_hT, 1)
                    leaky(0, 0)
                    keep_transposed(0, 0)

                    def body(t, b, k):
                        if not (isinstance(t, int) and t == LAST):
                            leaky(t + 1, 1 - b)
                            keep_transposed(t + 1, 1 - b)
                        v.wait_ge(e_ps, t + (o + 1))
                        nc.vector.tensor_tensor(row(acc, t), psum[4 + b][:, :], bias[:, :],
                                                ALU.add).then_inc(e_s, 1)
                    row_tiles(v, body)

                @block.tensor
                def _(pe):
                    def turn(t, b):
                        pe.wait_ge(e_h, t + (o + 1))
                        need(pe, e_hT, t + (o - 1))
                        for c in range(KB):
                            last = nc.tensor.transpose(part(psum[b], c), part(h[b], c), ident[:, :])
                        last.then_inc(e_pT, 1)
                    turn(0, 0)

                    def body(t, b, k):
                        pe.wait_ge(e_hT, t + (o + 1))
                        need(pe, e_g, t + (o - 1))
                        for c in range(KB):
                            last = nc.tensor.matmul(psum[2 + b][:, :], part(hT[b], c), wn_sb[:, c, :],
                                                    start=(c == 0), stop=(c == KB - 1))
                        last.then_inc(e_pg, 1)
                        if not (isinstance(t, int) and t == LAST):
                            turn(t + 1, 1 - b)
                        need(pe, e_s, t + (o - 1))
                        for c in range(KB):
                            last = nc.tensor.matmul(psum[4 + b][:, :], part(hT[b], c), ws_sb[:, c, :],
                                                    start=(c == 0), stop=(c == KB - 1))
                        last.then_inc(e_ps, 1)
                    row_tiles(pe, body)

        for l in range(LAYERS):
            if l:
                dense(l)
            aggregate(l)

        plan = Plan(0)
        w1_sb = plan.take(EXPERTS, KB, F)
        w2_sb = plan.take(EXPERTS, FB, C)
        AFTER_W = plan.at
        xin = [plan.take(C) for _ in range(2)]
        qin = [plan.take(C) for _ in range(2)]
        x1T = [plan.take(C) for _ in range(2)]
        part_sum, h3, xn1 = plan.take(C), plan.take(C), plan.take(C)
        z, stat1, mv1 = plan.take(2), plan.take(6), plan.take(2)
        f_in = [sem(f"f_in{b}") for b in range(2)]
        f_st = [sem(f"f_st{b}") for b in range(2)]
        f_w, f_po, f_v, f_pow, f_xn, f_pT, f_xT, f_pl, f_l = (sem("f_" + n) for n in
                                                             "w po v pow xn pT xT pl l".split())

        with nc.Block() as block:
            @block.sync
            def _(sp):
                for e in range(EXPERTS):
                    sp.dma_start(w1_sb[:, e, :, :], w1[e].rearrange("(k p) f -> p k f", p=P)).then_inc(f_w, 16)
                    sp.dma_start(w2_sb[:, e, :, :], w2[e].rearrange("(k p) f -> p k f", p=P)).then_inc(f_w, 16)

                def load(t, b, k):
                    need(sp, f_xn, t - 1)
                    sp.dma_start(xin[b][:, :], dram_tile(x_t, t)).then_inc(f_in[b], 16)
                    sp.dma_start(qin[b][:, :], dram_tile(q_tab, t)).then_inc(f_in[b], 16)

                row_tiles(sp, load)
                sp.wait_ge(f_w, 16 * 2 * EXPERTS)

            @block.scalar
            def _(act):
                def keep_transposed(t, b, k):
                    act.wait_ge(f_pT, t + 1)
                    need(act, f_st[b], 16 * k)
                    need(act, f_pl, t - 1)
                    nc.scalar.copy(x1T[b][:, :], psum[4 + b][:, :]).then_inc(f_xT, 1)
                    act.wait_ge(f_xT, t + 1)
                    act.dma_start(dram_tile(xt_tab, t), x1T[b][:, :]).then_inc(f_st[b], 16)
                row_tiles(act, keep_transposed)
                for b in range(2):
                    act.wait_ge(f_st[b], 16 * (NT // 2 + (1 - b) * (NT % 2)))

            @block.gpsimd
            def _(pool):
                def power(t, b, k):
                    pool.wait_ge(f_v, 8 * t + 8)
                    nc.gpsimd.tensor_tensor(rstd[:, ds(t, 1)], rstd[:, ds(t, 1)], half[:, 0:1],
                                            ALU.pow).then_inc(f_pow, 1)
                row_tiles(pool, power)

            @block.vector
            def _(v):
                def body(t, b, k):
                    done = [8 * t]

                    def step(ins, wait=need):
                        ins.then_inc(f_v, 1)
                        done[0] = done[0] + 1
                        wait(v, f_v, done[0])
                    v.wait_ge(f_in[b], 32 * k + 32)
                    v.wait_ge(f_po, t + 1)
                    step(nc.vector.tensor_scalar(z[:, 0:1], psum[2 + b][:, 0:1], MIX_EPS, None, ALU.add))
                    step(nc.vector.reciprocal(z[:, 1:2], z[:, 0:1]))
                    nc.vector.scalar_tensor_tensor(h3[:, :], row(acc, t), SLOPE, row(acc, t), ALU.mult, ALU.max)
                    step(nc.vector.scalar_tensor_tensor(part_sum[:, :], psum[b][:, :], z[:, 1:2], xin[b][:, :],
                                                        ALU.mult, ALU.add))
                    step(nc.vector.tensor_tensor(row(acc, t), part_sum[:, :], h3[:, :], ALU.add), gate)
                    step(nc.vector.bn_stats(stat1[:, :], row(acc, t)), gate)
                    step(nc.vector.bn_aggr(mv1[:, :], stat1[:, :]))
                    step(nc.vector.tensor_copy(row(mv, t), mv1[:, :]))
                    step(nc.vector.tensor_scalar(rstd[:, ds(t, 1)], row(mv, t)[:, 1:2], LN_EPS, None, ALU.add))
                    v.wait_ge(f_pow, t + 1)
                    need(v, f_pT, t)
                    nc.vector.tensor_scalar(xn1[:, :], row(acc, t), row(mv, t)[:, 0:1], rstd[:, ds(t, 1)],
                                            ALU.subtract, ALU.mult).then_inc(f_xn, 1)
                    v.wait_ge(f_pl, t + 1)
                    nc.vector.tensor_tensor(row(logits, t), psum[6 + b][:, 0:EXPERTS], bg_sb[:, :],
                                            ALU.add).then_inc(f_l, 1)
                row_tiles(v, body)

            @block.tensor
            def _(pe):
                def body(t, b, k):
                    pe.wait_ge(f_in[b], 32 * k + 32)
                    need(pe, f_l, t - 1)
                    for d in range(KB):
                        nc.tensor.matmul(psum[2 + b][:, 0:1], part(qin[b], d), ksum[:, d:d + 1],
                                         start=(d == 0), stop=(d == KB - 1))
                    for d in range(KB):
                        last = nc.tensor.matmul(psum[b][:, :], part(qin[b], d), kv[:, d, :],
                                                start=(d == 0), stop=(d == KB - 1))
                    last.then_inc(f_po, 1)
                    pe.wait_ge(f_xn, t + 1)
                    need(pe, f_xT, t - 1)
                    for c in range(KB):
                        last = nc.tensor.transpose(part(psum[4 + b], c), part(xn1, c), ident[:, :])
                    last.then_inc(f_pT, 1)
                    pe.wait_ge(f_xT, t + 1)
                    for c in range(KB):
                        last = nc.tensor.matmul(psum[6 + b][:, 0:EXPERTS], part(x1T[b], c), wg_sb[:, c, :],
                                                start=(c == 0), stop=(c == KB - 1))
                    last.then_inc(f_pl, 1)
                row_tiles(pe, body)

        plan = Plan(AFTER_W)
        cnt, cmp = plan.take(NT, EXPERTS), plan.take(NT, EXPERTS)
        top, tot = plan.take(NT), plan.take(NT)
        b1_sb = plan.take(EXPERTS * FB)
        b2_sb = plan.take(C)
        g_v, g_a, g_ld = sem("g_v"), sem("g_a"), sem("g_ld")

        def over_experts(ap):
            return ap[:, :].unsqueeze(2).to_broadcast([P, NT, EXPERTS])

        with nc.Block() as block:
            @block.sync
            def _(sp):
                sp.dma_start(b1_sb[:, :], b1[:, :]).then_inc(g_ld, 16)
                sp.dma_start(b2_sb[0:EXPERTS, :], b2[:, :]).then_inc(g_ld, 16)
                sp.wait_ge(g_ld, 32)

            @block.scalar
            def _(act):
                act.wait_ge(g_v, 2)
                nc.scalar.activation(logits[:, :, :], logits[:, :, :], ACT.Exp).then_inc(g_a, 1)

            @block.vector
            def _(v):
                done = [0]

                def step(ins):
                    ins.then_inc(g_v, 1)
                    done[0] += 1
                    v.wait_ge(g_v, done[0])
                step(nc.vector.tensor_reduce(top[:, :], logits[:, :, :], AX.X, ALU.max))
                step(nc.vector.tensor_tensor(logits[:, :, :], logits[:, :, :], over_experts(top), ALU.subtract))
                v.wait_ge(g_a, 1)
                step(nc.vector.tensor_reduce(tot[:, :], logits[:, :, :], AX.X, ALU.add))
                step(nc.vector.reciprocal(tot[:, :], tot[:, :]))
                step(nc.vector.tensor_tensor(logits[:, :, :], logits[:, :, :], over_experts(tot), ALU.mult))
                step(nc.vector.memset(cnt[:, :, :], 0.0))
                for j in range(EXPERTS):
                    pj = logits[:, :, j:j + 1]
                    if j:
                        nc.vector.tensor_tensor(cmp[:, :, 0:j], logits[:, :, 0:j],
                                                pj.to_broadcast([P, NT, j]), ALU.is_lt)
                    n = EXPERTS - 1 - j
                    if n:
                        nc.vector.tensor_tensor(cmp[:, :, j + 1:], logits[:, :, j + 1:],
                                                pj.to_broadcast([P, NT, n]), ALU.is_le)
                    step(nc.vector.memset(cmp[:, :, j:j + 1], 0.0))
                    step(nc.vector.tensor_tensor(cnt[:, :, :], cnt[:, :, :], cmp[:, :, :], ALU.add))
                step(nc.vector.tensor_scalar(cnt[:, :, :], cnt[:, :, :], 1.5, None, ALU.is_lt))
                step(nc.vector.tensor_tensor(comb[:, :, :], logits[:, :, :], cnt[:, :, :], ALU.mult))

        xp = [plan.take(KB, 2 * P) for _ in range(2)]
        hm = [plan.take(FB, 2 * P) for _ in range(2)]
        combT = plan.take(2, P)
        cpair = plan.take(2, EXPERTS)
        h_in = [sem(f"h_in{b}") for b in range(2)]
        h_pu, h_h, h_pd, h_acc, h_pc, h_c, h_out = (sem("h_" + n) for n in "pu h pd acc pc c out".split())
        PAIRS = NT // 2

        with nc.Block() as block:
            def pairs(eng, body):
                body(0, 0, 0, 2)
                body(1, 1, 0, 2)
                with eng.Fori(1, PAIRS // 2) as i:
                    body(2 * i, 0, i, 2)
                    body(2 * i + 1, 1, i, 2)
                body(PAIRS, 0, PAIRS // 2, 1)

            PER = 2 * (EXPERTS + 1)

            @block.sync
            def _(sp):
                def load(q, b, k, tiles):
                    need(sp, h_pu, (q - 1) * EXPERTS)
                    for a in range(tiles):
                        sp.dma_start(xp[b][:, :, a * P:(a + 1) * P],
                                     dram_tile(xt_tab, 2 * q + a).rearrange("p (k n) -> p k n", k=KB)
                                     ).then_inc(h_in[b], 16)
                pairs(sp, load)

            h_gate, h_pb, h_cc = sem("h_gate"), sem("h_pb"), sem("h_cc")

            @block.gpsimd
            def _(pool):
                def store(q, b, k, tiles):
                    pool.wait_ge(h_acc, q * PER + (EXPERTS + 1) * tiles)
                    pool.sem_inc(h_gate, 1)
                    for a in range(tiles):
                        pool.dma_start(dram_tile(out_t, 2 * q + a), row(acc, 2 * q + a)).then_inc(h_out, 16)
                pairs(pool, store)
                pool.wait_ge(h_out, 16 * NT)

            @block.scalar
            def _(act):
                def body(q, b, k, tiles):
                    for e in range(EXPERTS):
                        n = q * EXPERTS + e
                        act.wait_ge(h_pu, n + 1)
                        need(act, h_pd, n - 1)
                        for f in range(FB):
                            last = nc.scalar.activation(
                                hm[e % 2][:, f, 0:tiles * P],
                                psum[e % 2][:, f * 2 * P:f * 2 * P + tiles * P],
                                ACT.Gelu_apprx_tanh, bias=b1_sb[:, e * FB + f:e * FB + f + 1])
                        last.then_inc(h_h, 1)
                pairs(act, body)

            @block.vector
            def _(v):
                def body(q, b, k, tiles):
                    nc.vector.tensor_copy(cpair[:, 0:tiles, :], comb[:, ds(2 * q, tiles), :]).then_inc(h_cc, 1)
                    v.wait_ge(h_pc, q + 1)
                    nc.vector.tensor_copy(combT[0:EXPERTS, 0:tiles, :],
                                          psum[6][0:EXPERTS, 0:tiles * P].rearrange("p (a n) -> p a n", a=tiles)
                                          ).then_inc(h_c, 1)
                    for e in range(EXPERTS):
                        v.wait_ge(h_pd, q * EXPERTS + e + 1)
                        if e:
                            v.wait_ge(h_acc, q * PER + e * tiles)
                        for a in range(tiles):
                            at = row(acc, 2 * q + a)
                            nc.vector.scalar_tensor_tensor(at, psum[2 + 2 * (e % 2) + a][:, :],
                                                           row(comb, 2 * q + a)[:, e:e + 1], at,
                                                           ALU.mult, ALU.add).then_inc(h_acc, 1)
                    v.wait_ge(h_acc, q * PER + EXPERTS * tiles)
                    for a in range(tiles):
                        v.wait_ge(h_pb, 2 * q + a + 1)
                        at = row(acc, 2 * q + a)
                        nc.vector.tensor_tensor(at, psum[7][:, :], at, ALU.add).then_inc(h_acc, 1)
                pairs(v, body)

            @block.tensor
            def _(pe):
                def up(q, b, e, tiles):
                    need(pe, h_h, q * EXPERTS + e - 1)
                    for f in range(FB):
                        for c in range(KB):
                            last = nc.tensor.matmul(psum[e % 2][:, f * 2 * P:f * 2 * P + tiles * P],
                                                    w1_sb[:, e, c, f * P:(f + 1) * P], xp[b][:, c, 0:tiles * P],
                                                    start=(c == 0), stop=(c == KB - 1))
                    last.then_inc(h_pu, 1)

                def down(q, e, tiles):
                    pe.wait_ge(h_h, q * EXPERTS + e + 1)
                    if e >= 2:
                        pe.wait_ge(h_acc, q * PER + (e - 1) * tiles)
                    else:
                        need(pe, h_acc, q * PER)
                    for a in range(tiles):
                        for f in range(FB):
                            last = nc.tensor.matmul(psum[2 + 2 * (e % 2) + a][:, :],
                                                    hm[e % 2][:, f, a * P:(a + 1) * P], w2_sb[:, e, f, :],
                                                    start=(f == 0), stop=(f == FB - 1))
                    last.then_inc(h_pd, 1)

                def body(q, b, k, tiles):
                    pe.wait_ge(h_in[b], 32 * k + 16 * tiles)
                    up(q, b, 0, tiles)
                    pe.wait_ge(h_cc, q + 1)
                    for a in range(tiles):
                        last = nc.tensor.transpose(psum[6][0:EXPERTS, a * P:(a + 1) * P], cpair[:, a, :],
                                                   ident[:, :])
                    last.then_inc(h_pc, 1)
                    for e in range(EXPERTS):
                        if e + 1 < EXPERTS:
                            up(q, b, e + 1, tiles)
                        down(q, e, tiles)
                    for a in range(tiles):
                        pe.wait_ge(h_c, q + 1)
                        need(pe, h_acc, q * PER if a == 0 else q * PER + EXPERTS * tiles + 1)
                        last = nc.tensor.matmul(psum[7][:, :], combT[0:EXPERTS, a, :], b2_sb[0:EXPERTS, :],
                                                start=True, stop=True)
                        last.then_inc(h_pb, 1)
                pairs(pe, body)


def kernel(x, src, dst, **w):
    import numpy as np
    import concourse.bacc as bacc
    from concourse.bass_utils import run_bass_kernel_spmd as run

    xp = np.concatenate([x, np.zeros((NPAD - N, C), np.float32)])
    pad = EPAD - E
    s = np.concatenate([src, np.zeros(pad, np.int32)])
    d = np.concatenate([dst, np.full(pad, NPAD - 1, np.int32)])
    a = {
        "x": xp,
        "src": s.reshape(NE, P).T,
        "dst": d.reshape(NE, P).T,
        "dstg": d.reshape(NG // 2, 2, GT * P),
        "ws": np.stack([np.stack([w[f"L0_gnn_w_self{i}"] for i in range(LAYERS)]),
                        np.stack([w[f"L0_gnn_w_neigh{i}"] for i in range(LAYERS)])]),
        "bs": np.stack([w[f"L0_gnn_b{i}"] for i in range(LAYERS)]),
        "wqk": np.asarray(w["L0_mix_W_qk"]).T,
        "wg": w["L0_ffn_Wg"], "bg": w["L0_ffn_bg"],
        "w1": w["L0_ffn_W1"],
        "b1": np.asarray(w["L0_ffn_b1"]).reshape(EXPERTS * FB, P).T,
        "w2": w["L0_ffn_W2"], "b2": w["L0_ffn_b2"],
    }
    a = {k: np.ascontiguousarray(v) for k, v in a.items()}
    nc = bacc.Bacc("TRN2", target_bir_lowering=False, num_devices=1)
    args = {k: nc.dram_tensor("in_" + k, v.shape, mybir.dt.from_np(v.dtype), kind="ExternalInput").ap()
            for k, v in a.items()}
    out = nc.dram_tensor("out", (NPAD, C), mybir.dt.float32, kind="ExternalOutput").ap()
    build_kernel(nc, out=out, **args)
    r = run(nc, [{"in_" + k: v for k, v in a.items()}], core_ids=[0])
    return r.results[0]["out"][:N]
```

```python
import concourse.bass as bass
from concourse import mybir
from contextlib import ExitStack

P = 128
C = 512
KB = C // P
N = 6250
NT = -(-N // P)
NPAD = NT * P
E = 100000
GT = 4
TURN = 4
NG = -(-E // (P * GT * TURN)) * TURN
NE = NG * GT
EPAD = NE * P
HALVES = NG // 2
RAW = 2 * GT
LAYERS = 3
EXPERTS = 8
F = 256
FB = F // P
LN_EPS = 1e-5
MIX_EPS = 1e-6
SLOPE = 0.01
LAST = NT - 1
SHIFT = P.bit_length() - 1
UNIT = KB * C
WN, WQ, WK = LAYERS, 2 * LAYERS, 2 * LAYERS + 1
FARENA = 10 * C


def build_kernel(nc, x, src, dst, dstg, w512, bs, wg, bg, w1, b1, w2, b2, out):
    f32, f32r, i32, bf16 = mybir.dt.float32, mybir.dt.float32r, mybir.dt.int32, mybir.dt.bfloat16
    ALU = mybir.AluOpType
    ACT = mybir.ActivationFunctionType
    AX = mybir.AxisListType
    ds = bass.ds

    def dram(name, shape, dt=f32):
        return nc.dram_tensor(name, shape, dt, kind="Internal").ap()

    g_tab = [dram(f"g_tab{i}", (NPAD, C)) for i in range(2)]
    q_tab = dram("q_tab", (NT, P, C))
    kv_tab = dram("kv_tab", (P, KB * C))
    x1_tab = dram("x1_tab", (NT, P, C))
    x1T_tab = dram("x1T_tab", (NT, P, 2 * C), f32r)

    x_t = x.rearrange("(t p) f -> t p f", p=P)
    out_t = out.rearrange("(t p) f -> t p f", p=P)

    ctx = ExitStack()
    with ctx:
        def sb(name, shape, dt=f32, scope=ctx):
            return scope.enter_context(nc.sbuf_tensor(name, shape, dt))

        def sem(name):
            return ctx.enter_context(nc.semaphore(name))

        ident = sb("ident", [P, P])
        iota = sb("iota", [P, P])
        wbase = sb("wbase", [P, NT])
        ones = sb("ones", [P, 2])
        half = sb("half", [P, NT])
        rdeg = sb("rdeg", [P, NT])
        wlo = sb("wlo", [1, NG], i32)
        whi = sb("whi", [1, NG], i32)
        extra = sb("extra", [1, NG + 1], i32)
        mv = sb("mv", [P, NT, 2])
        rstd = sb("rstd", [P, NT])
        comb = sb("comb", [P, NT, EXPERTS])
        psum = [ctx.enter_context(nc.psum_tensor(f"psum{i}", [P, C], f32)) for i in range(8)]
        s_gate = sem("s_gate")

        class Plan:
            def __init__(self, tensor, at=0):
                self.tensor, self.at, self.size = tensor, at, tensor.shape[1]

            def take(self, *shape):
                n = 1
                for s in shape:
                    n *= s
                ap = self.tensor[:, self.at:self.at + n]
                self.at += n
                assert self.at <= self.size, (self.at, self.size)
                if len(shape) == 2:
                    ap = ap.rearrange("p (a b) -> p a b", a=shape[0])
                if len(shape) == 3:
                    ap = ap.rearrange("p (a b c) -> p a b c", a=shape[0], b=shape[1])
                return ap

        def row_tiles(eng, body):
            body(0, 0, 0)
            body(1, 1, 0)
            with eng.Fori(1, NT // 2) as i:
                body(2 * i, 0, i)
                body(2 * i + 1, 1, i)
            body(NT - 1, 0, NT // 2)

        def turns(b):
            return NT // 2 + (1 - b) * (NT % 2)

        def need(eng, sem, n):
            if not isinstance(n, int) or n > 0:
                eng.wait_ge(sem, n)

        def gate(eng, sem, n):
            if not isinstance(n, int) or n > 0:
                eng.wait_ge(sem, n)
                eng.sem_inc(s_gate, 1)

        def row(ap, t):
            return ap[:, ds(t, 1), :].rearrange("p a f -> p (a f)")

        def dram_tile(ap, t):
            return ap[ds(t, 1), :, :].rearrange("a p f -> (a p) f")

        def part(ap, k):
            return ap[:, k * P:(k + 1) * P]

        def plain(ap):
            return ap.bitcast(f32)

        def product(to, left, right, first=True, final=True):
            n = len(left)
            for c in range(n):
                (lh, ll), (rh, rl) = left[c], right[c]
                nc.tensor.matmul(to, lh, rh, start=first and c == 0, stop=False)
                nc.tensor.matmul(to, lh, rl, start=False, stop=False)
                last = nc.tensor.matmul(to, ll, rh, start=False, stop=final and c == n - 1)
            return last

        def blocks(pair):
            return [(part(pair[:, 0, :], k), part(pair[:, 1, :], k)) for k in range(KB)]

        def weight(w, lo=0, width=C):
            return [(w[:, 0, k * C + lo:k * C + lo + width], w[:, 1, k * C + lo:k * C + lo + width])
                    for k in range(KB)]

        graph = ExitStack()
        acc = sb("acc", [P, NT, C], f32, graph)
        dneg = sb("dneg", [P, NE], f32, graph)
        farena = sb("farena", [P, FARENA], f32, graph)
        wn_r = sb("wn_r", [P, 2, UNIT], f32r, graph)
        ws_r = sb("ws_r", [P, 2, UNIT], f32r, graph)
        ksum = sb("ksum", [P, KB], f32, graph)

        pre = ExitStack()
        GP = NG // 2
        di = sb("di", [P, NE], i32, pre)
        dg_i = sb("dg_i", [P, 2, C], i32, pre)
        dg_f = sb("dg_f", [P, 2, C], f32, pre)
        lohi_i = sb("lohi_i", [P, 4], i32, pre)
        lohi_f = sb("lohi_f", [P, 4], f32, pre)
        nextra = sb("nextra", [P, 2], f32, pre)
        upto = sb("upto", [P, 2, NG + 1], f32, pre)
        pick = sb("pick", [P, 2, NG], f32, pre)
        stat = sb("stat", [P, 2, 6], f32, pre)
        mvt = sb("mvt", [P, 2, 2], f32, pre)
        dr_i = sb("dr_i", [P, NE], i32, pre)
        dw_i = sb("dw_i", [P, NE], i32, pre)
        dr = sb("dr", [P, NE], f32, pre)
        dw = sb("dw", [P, NE], f32, pre)
        hot_r = sb("hot_r", [P, 2, GT, P], bf16, pre)
        hot_w = sb("hot_w", [P, 2, GT, NT], bf16, pre)
        s_ld, s_x, s_c, s_v, s_st, s_pt, s_pool, s_bn = (sem(n) for n in
            ("s_ld", "s_x", "s_c", "s_v", "s_st", "s_pt", "s_pool", "s_bn"))
        s_hot, s_deg = sem("s_hot"), sem("s_deg")
        XCH = 7

        with pre, nc.Block() as block:
            @block.sync
            def _(sp):
                sp.dma_start(di[:, :], dst[:, :]).then_inc(s_ld, 16)
                sp.dma_start(dg_i[0:GP, :, :], dstg[:, :, :]).then_inc(s_ld, 16)
                with sp.Fori(0, NT // XCH) as i:
                    sp.dma_start(acc[:, ds(i * XCH, XCH), :],
                                 x_t[ds(i * XCH, XCH), :, :].rearrange("t p f -> p t f")).then_inc(s_x, 16)

            @block.gpsimd
            def _(pool):
                nc.gpsimd.iota(iota[:, :], pattern=[[1, P]], base=0, channel_multiplier=0,
                               allow_small_or_imprecise_dtypes=True)
                nc.gpsimd.iota(wbase[:, :], pattern=[[P, NT]], base=0, channel_multiplier=0,
                               allow_small_or_imprecise_dtypes=True)
                nc.gpsimd.memset(ones[:, :], 1.0)
                nc.gpsimd.memset(half[:, :], -0.5)
                nc.gpsimd.memset(ident[:, :], 0.0).then_inc(s_c, 1)
                nc.gpsimd.memset(upto[:, :, :], 1.0).then_inc(s_c, 1)
                nc.gpsimd.memset(pick[:, :, :], 0.0).then_inc(s_c, 1)
                pool.wait_ge(s_c, 3)
                nc.gpsimd.affine_select(out=ident[:, :], in_=ident[:, :], compare_op=ALU.not_equal, fill=1.0,
                                        base=0, pattern=[[-1, P]], channel_multiplier=1)
                nc.gpsimd.affine_select(out=upto[:, :, :], in_=upto[:, :, :], compare_op=ALU.is_gt, fill=0.0,
                                        base=0, pattern=[[-1, 2], [1, NG + 1]], channel_multiplier=-2)
                nc.gpsimd.affine_select(out=pick[:, :, :], in_=pick[:, :, :], compare_op=ALU.not_equal, fill=1.0,
                                        base=0, pattern=[[1, 2], [-1, NG]],
                                        channel_multiplier=2).then_inc(s_pool, 1)
                pool.wait_ge(s_st, NT + 1)
                nc.gpsimd.tensor_tensor(rstd[:, :], rstd[:, :], half[:, :], ALU.pow).then_inc(s_pool, 1)

            @block.vector
            def _(v):
                done = [0]

                def step(ins):
                    ins.then_inc(s_v, 1)
                    done[0] += 1
                    v.wait_ge(s_v, done[0])
                v.wait_ge(s_ld, 32)
                nc.vector.tensor_scalar(dneg[:, :], di[:, :], -1.0, None, ALU.mult)
                step(nc.vector.tensor_copy(dg_f[0:GP, :, :], dg_i[0:GP, :, :]))
                nc.vector.tensor_reduce(lohi_f[0:GP, 0:2], dg_f[0:GP, :, :], AX.X, ALU.min)
                step(nc.vector.tensor_reduce(lohi_f[0:GP, 2:4], dg_f[0:GP, :, :], AX.X, ALU.max))
                step(nc.vector.tensor_copy(lohi_i[0:GP, :], lohi_f[0:GP, :]))
                step(nc.vector.tensor_scalar(lohi_i[0:GP, :], lohi_i[0:GP, :], SHIFT, None,
                                             ALU.arith_shift_right))
                step(nc.vector.tensor_copy(lohi_f[0:GP, :], lohi_i[0:GP, :]))
                step(nc.vector.tensor_tensor(nextra[0:GP, :], lohi_f[0:GP, 2:4], lohi_f[0:GP, 0:2],
                                             ALU.subtract))
                v.wait_ge(s_pt, 1)
                nc.vector.tensor_copy(extra[0:1, :], psum[0][0:1, 0:NG + 1])
                nc.vector.tensor_copy(wlo[0:1, :], psum[1][0:1, 0:NG])
                nc.vector.tensor_copy(whi[0:1, :], psum[3][0:1, 0:NG])

                nc.vector.tensor_scalar(dr_i[:, :], di[:, :], P - 1, None, ALU.bitwise_and)
                step(nc.vector.tensor_scalar(dw_i[:, :], di[:, :], SHIFT, None, ALU.arith_shift_right))
                nc.vector.tensor_copy(dr[:, :], dr_i[:, :])
                step(nc.vector.tensor_copy(dw[:, :], dw_i[:, :]))
                v.wait_ge(s_pool, 1)

                def hots(g, b):
                    need(v, s_deg, g - 1)
                    nc.vector.tensor_tensor(hot_r[:, b, :, :],
                                            iota[:, :].unsqueeze(1).to_broadcast([P, GT, P]),
                                            dr[:, ds(g * GT, GT)].unsqueeze(2).to_broadcast([P, GT, P]),
                                            ALU.is_equal)
                    nc.vector.tensor_tensor(hot_w[:, b, :, :],
                                            iota[:, 0:NT].unsqueeze(1).to_broadcast([P, GT, NT]),
                                            dw[:, ds(g * GT, GT)].unsqueeze(2).to_broadcast([P, GT, NT]),
                                            ALU.is_equal).then_inc(s_hot, 1)
                hots(0, 0)
                hots(1, 1)
                with v.Fori(1, NG // 2) as i:
                    hots(2 * i, 0)
                    hots(2 * i + 1, 1)
                v.wait_ge(s_deg, NG)
                step(nc.vector.tensor_scalar(rdeg[:, :], psum[2][:, 0:NT], 1.0, None, ALU.max))
                step(nc.vector.reciprocal(rdeg[:, :], rdeg[:, :]))

                def stats(t, b, k):
                    gate(v, s_st, t - 1)
                    nc.vector.bn_stats(stat[:, b, :], row(acc, t)).then_inc(s_bn, 1)
                    gate(v, s_bn, 2 * t + 1)
                    nc.vector.bn_aggr(mvt[:, b, :], stat[:, b, :]).then_inc(s_bn, 1)
                    v.wait_ge(s_bn, 2 * t + 2)
                    nc.vector.tensor_copy(row(mv, t), mvt[:, b, :]).then_inc(s_st, 1)
                v.wait_ge(s_x, 16 * (NT // XCH))
                row_tiles(v, stats)
                v.wait_ge(s_st, NT)
                nc.vector.tensor_scalar(rstd[:, :], mv[:, :, 1], LN_EPS, None, ALU.add).then_inc(s_st, 1)
                v.wait_ge(s_pool, 2)

            @block.tensor
            def _(pe):
                pe.wait_ge(s_v, 6)
                pe.wait_ge(s_pool, 1)
                for bank, values, which in ((0, nextra[:, 0:2], upto), (1, lohi_f[:, 0:2], pick),
                                            (3, lohi_f[:, 2:4], pick)):
                    for j in range(2):
                        last = nc.tensor.matmul(psum[bank][0:1, 0:which.shape[2]], values[0:GP, j:j + 1],
                                                which[0:GP, j, :], start=(j == 0), stop=(j == 1))
                last.then_inc(s_pt, 1)

                def count(g, b, first=False, final=False):
                    pe.wait_ge(s_hot, g + 1)
                    for j in range(GT):
                        last = nc.tensor.matmul(psum[2][:, 0:NT], hot_r[:, b, j, :], hot_w[:, b, j, :],
                                                start=first and j == 0, stop=final and j == GT - 1)
                    last.then_inc(s_deg, 1)
                count(0, 0, first=True)
                count(1, 1)
                with pe.Fori(1, NG // 2 - 1) as i:
                    count(2 * i, 0)
                    count(2 * i + 1, 1)
                count(NG - 2, 0)
                count(NG - 1, 1, final=True)


        stage = [farena[:, i * UNIT:(i + 1) * UNIT] for i in range(2)]
        w_in = [sem(f"w_in{b}") for b in range(2)]
        w_hi, w_lo = sem("w_hi"), sem("w_lo")

        def load_weights(units, o):
            with nc.Block() as block:
                @block.sync
                def _(sp):
                    for u, (source, to) in enumerate(units):
                        need(sp, w_lo, u + o - 1 if u > 1 else 0)
                        sp.dma_start(stage[u % 2].rearrange("p (k f) -> p k f", k=KB),
                                     source.rearrange("(k p) f -> p k f", p=P)).then_inc(w_in[u % 2], 16)

                @block.scalar
                def _(act):
                    for u, (source, to) in enumerate(units):
                        act.wait_ge(w_in[u % 2], 16 * ((u + o) // 2 + 1))
                        nc.scalar.copy(to[:, 0, :], stage[u % 2]).then_inc(w_hi, 1)

                @block.vector
                def _(v):
                    for u, (source, to) in enumerate(units):
                        v.wait_ge(w_hi, u + o + 1)
                        nc.vector.tensor_tensor(to[:, 1, :], stage[u % 2], plain(to[:, 0, :]),
                                                ALU.subtract).then_inc(w_lo, 1)
                    v.wait_ge(w_lo, len(units) + o)

        first = ExitStack()
        wk_r = sb("wk_r", [P, 2, UNIT], f32r, first)
        wq_r = sb("wq_r", [P, 2, UNIT], f32r, first)
        load_weights([(w512[0], ws_r), (w512[WN], wn_r), (w512[WQ], wq_r), (w512[WK], wk_r)], 0)
        xT = [sb(f"xT{b}", [P, 2, C], f32r, first) for b in range(2)]
        plan = Plan(farena)
        xn = [plan.take(C) for _ in range(2)]
        gbuf = [plan.take(C) for _ in range(2)]
        kbuf = [plan.take(C) for _ in range(2)]
        qbuf, kacc, bias = plan.take(C), plan.take(C), plan.take(C)
        ek = plan.take(C)
        eq = ek
        kvbuf = farena[:, 0:UNIT]
        tT, tK, tG, tS, tQ = psum[4], psum[5], psum[6], psum[7], psum[5]
        (s_b, s_xn, s_k, s_hi, s_lo, s_s, s_q, s_e, s_g, s_pk, s_pg, s_pT, s_ps, s_pq, s_pkv, s_kacc, s_m,
         s_kv) = (sem("c_" + n) for n in "b xn k hi lo s q e g pk pg pT ps pq pkv kacc m kv".split())
        s_gst = [sem(f"c_gst{b}") for b in range(2)]
        s_qst = sem("c_qst")

        with first, nc.Block() as block:
            @block.sync
            def _(sp):
                sp.dma_start(bias[:, :], bs[0].partition_broadcast(P)).then_inc(s_b, 16)

                def store(t, b, k):
                    sp.wait_ge(s_g, t + 1)
                    sp.dma_start(g_tab[0][ds(t * P, P), :], gbuf[b][:, :]).then_inc(s_gst[b], 16)
                    sp.wait_ge(s_q, t + 1)
                    sp.dma_start(dram_tile(q_tab, t), qbuf[:, :]).then_inc(s_qst, 16)
                row_tiles(sp, store)
                for b in range(2):
                    sp.wait_ge(s_gst[b], 16 * turns(b))
                sp.wait_ge(s_qst, 16 * NT)
                sp.wait_ge(s_kv, 1)
                sp.dma_start(kv_tab[:, :], kvbuf).then_inc(s_kv, 16)
                sp.wait_ge(s_kv, 17)

            @block.gpsimd
            def _(pool):
                nc.gpsimd.memset(kacc[:, :], 0.0).then_inc(s_kacc, 1)

                def add_keys(t, b, k):
                    pool.wait_ge(s_k, t + 1)
                    pool.wait_ge(s_kacc, t + 1)
                    rows = N - LAST * P if isinstance(t, int) and t == LAST else P
                    nc.gpsimd.tensor_tensor(kacc[0:rows, :], kacc[0:rows, :], kbuf[b][0:rows, :],
                                            ALU.add).then_inc(s_kacc, 1)
                row_tiles(pool, add_keys)

            @block.scalar
            def _(act):
                def exp_negative(bank, m):
                    nc.scalar.activation(ek[:, :], bank[:, :], ACT.Relu, scale=-1.0).then_inc(s_m, 1)
                    act.wait_ge(s_m, m)
                    nc.scalar.activation(ek[:, :], ek[:, :], ACT.Exp, scale=-1.0).then_inc(s_e, 1)

                def keep_transposed(t, b):
                    act.wait_ge(s_pT, t + 1)
                    need(act, s_pq, t - 1)
                    nc.scalar.copy(xT[b][:, 0, :], tT[:, :]).then_inc(s_hi, 1)
                keep_transposed(0, 0)

                def body(t, b, k):
                    act.wait_ge(s_pk, t + 1)
                    need(act, s_q, t)
                    exp_negative(tK, 2 * t + 1)
                    act.wait_ge(s_pg, t + 1)
                    need(act, s_gst[b], 16 * k)
                    nc.scalar.copy(gbuf[b][:, :], tG[:, :]).then_inc(s_g, 1)
                    if not (isinstance(t, int) and t == LAST):
                        keep_transposed(t + 1, 1 - b)
                    act.wait_ge(s_pq, t + 1)
                    act.wait_ge(s_k, t + 1)
                    exp_negative(tQ, 2 * t + 2)
                row_tiles(act, body)

            @block.vector
            def _(v):
                def normalise(t, b):
                    need(v, s_pkv, t - 1)
                    nc.vector.tensor_scalar(xn[b][:, :], row(acc, t), row(mv, t)[:, 0:1],
                                            rstd[:, ds(t, 1)], ALU.subtract, ALU.mult).then_inc(s_xn, 1)

                def rest_transposed(t, b):
                    v.wait_ge(s_hi, t + 1)
                    nc.vector.tensor_tensor(xT[b][:, 1, :], tT[:, :], plain(xT[b][:, 0, :]),
                                            ALU.subtract).then_inc(s_lo, 1)

                def feature(bank, to, done):
                    nc.vector.scalar_tensor_tensor(to, bank[:, :], 0.0, ek[:, :], ALU.max,
                                                   ALU.add).then_inc(done, 1)

                normalise(0, 0)
                rest_transposed(0, 0)
                v.wait_ge(s_b, 16)

                def body(t, b, k):
                    more = not (isinstance(t, int) and t == LAST)
                    if more:
                        normalise(t + 1, 1 - b)
                    v.wait_ge(s_e, 2 * t + 1)
                    need(v, s_kacc, t)
                    need(v, s_pkv, t - 1)
                    feature(tK, kbuf[b][:, :], s_k)
                    if more:
                        rest_transposed(t + 1, 1 - b)
                    v.wait_ge(s_ps, t + 1)
                    nc.vector.tensor_tensor(row(acc, t), tS[:, :], bias[:, :], ALU.add).then_inc(s_s, 1)
                    v.wait_ge(s_e, 2 * t + 2)
                    need(v, s_qst, 16 * t)
                    feature(tQ, qbuf[:, :], s_q)
                row_tiles(v, body)
                v.wait_ge(s_pkv, NT + 1)
                v.wait_ge(s_gst[0], 16 * turns(0))
                v.wait_ge(s_gst[1], 16 * turns(1))
                nc.vector.tensor_copy(ksum[:, :], psum[4][:, 0:KB])
                for d in range(KB):
                    last = nc.vector.tensor_copy(kvbuf[:, d * C:(d + 1) * C], psum[d][:, :])
                last.then_inc(s_kv, 1)

            @block.tensor
            def _(pe):
                def turn(t, b):
                    pe.wait_ge(s_xn, t + 1)
                    need(pe, s_lo, t)
                    for c in range(KB):
                        last = nc.tensor.transpose(part(tT, c), part(xn[b], c), ident[:, :])
                    last.then_inc(s_pT, 1)

                turn(0, 0)

                def body(t, b, k):
                    more = not (isinstance(t, int) and t == LAST)
                    pe.wait_ge(s_lo, t + 1)
                    need(pe, s_q, t)
                    product(tK[:, :], blocks(xT[b]), weight(wk_r)).then_inc(s_pk, 1)
                    need(pe, s_g, t)
                    product(tG[:, :], blocks(xT[b]), weight(wn_r)).then_inc(s_pg, 1)
                    if more:
                        turn(t + 1, 1 - b)
                    need(pe, s_s, t)
                    product(tS[:, :], blocks(xT[b]), weight(ws_r)).then_inc(s_ps, 1)
                    pe.wait_ge(s_k, t + 1)
                    for d in range(KB):
                        last = product(part(tQ, d), weight(wq_r, d * P, P), blocks(xT[b]))
                    last.then_inc(s_pq, 1)
                    start = isinstance(t, int) and t == 0
                    for d in range(KB):
                        last = nc.tensor.matmul(psum[d][:, :], part(kbuf[b], d), xn[b][:, :],
                                                start=start, stop=not more)
                    last.then_inc(s_pkv, 1)
                row_tiles(pe, body)
                pe.wait_ge(s_kacc, NT + 1)
                for d in range(KB):
                    last = nc.tensor.matmul(psum[4][:, d:d + 1], part(kacc, d), ones[:, 0:1], start=True,
                                            stop=True)
                last.then_inc(s_pkv, 1)

        conv = ExitStack()
        split = sb("split", [P, 4, 2, 2 * C], f32r, conv)
        hot = sb("hot", [P, 2, GT, P], f32r, conv)
        hotx = sb("hotx", [P, GT, P], f32r, conv)
        near = sb("near", [P, 2, GT], f32, conv)
        nearx = sb("nearx", [P, GT], f32, conv)
        idx = sb("idx", [P, 2, 2 * GT], i32, conv)
        plan = Plan(farena)
        raw = plan.take(4, 2 * C)
        dist = plan.take(2, GT * P)
        plan = Plan(farena)
        h = [plan.take(C) for _ in range(2)]
        gout = [plan.take(C) for _ in range(2)]
        bias = plan.take(C)
        hT = [split[:, b, :, 0:C] for b in range(2)]

        a_raw = [sem(f"a_raw{b}") for b in range(4)]
        a_idx = [sem(f"a_idx{b}") for b in range(2)]
        a_near, a_dist, a_hot, a_hi, a_lo, a_used, a_acc = (
            sem("a_" + n) for n in "near dist hot hi lo used acc".split())

        def aggregate(l):
            tab = g_tab[l % 2]
            o = l * NG
            a_nearx, a_hotx, a_px, a_xacc = (sem(f"a{l}_" + n) for n in "nearx hotx px xacc".split())
            bankx = psum[2]

            def extras_before(eng, g):
                return eng.value_load(extra[0:1, ds(g, 1)], min_val=0, max_val=NG * NT)

            def groups(eng, body):
                for b in range(TURN):
                    body(b, b, 0)
                with eng.Fori(1, NG // TURN - 1) as i:
                    for b in range(TURN):
                        body(TURN * i + b, b, i)
                for b in range(TURN):
                    body(NG - TURN + b, b, NG // TURN - 1)

            with nc.Block() as block:
                @block.sync
                def _(sp):
                    def body(g, b, i):
                        if b % 2 == 0:
                            need(sp, a_hi, 2 * (g + o) - 4)
                            u = 2 * i + b // 2
                            sp.dma_start(idx[:, b // 2, :], src[ds(u, 1), :, :].rearrange("a p j -> (a p) j")
                                         ).then_inc(a_idx[b // 2], 16)
                    groups(sp, body)

                @block.gpsimd
                def _(pool):
                    def body(g, b, i):
                        if b % 2 == 0:
                            gate(pool, a_idx[b // 2], 16 * i + (16 * (o // TURN) + 16))
                        for half_of in range(2):
                            slot = 2 * (b % 2) + half_of
                            gate(pool, a_lo, 2 * g + (2 * o + half_of - 3))
                            for j in range(2):
                                at = GT * (b % 2) + 2 * half_of + j
                                nc.gpsimd.indirect_dma_start(
                                    out=raw[:, slot, j * C:(j + 1) * C], out_offset=None, in_=tab[:, :],
                                    in_offset=bass.IndirectOffsetOnAxis(ap=idx[:, b // 2, at:at + 1], axis=0),
                                ).then_inc(a_raw[slot], 16)
                    groups(pool, body)

                @block.scalar
                def _(act):
                    def matrices(g, s):
                        act.wait_ge(a_near, g + (o + 1))
                        need(act, a_hot, g + (o - 1))
                        for j in range(GT):
                            last = nc.scalar.activation(part(dist[:, s, :], j), iota[:, :], ACT.Abs,
                                                        bias=near[:, s, j:j + 1])
                        last.then_inc(a_dist, 1)
                        act.wait_ge(a_dist, g + (o + 1))
                        need(act, a_used, g + (o - 1))
                        nc.scalar.activation(hot[:, s, :, :].rearrange("p j n -> p (j n)"),
                                             dist[:, s, :], ACT.Relu, bias=1.0, scale=-1.0).then_inc(a_hot, 1)
                    matrices(0, 0)

                    def body(g, b, i):
                        need(act, a_used, g + (o - 1))
                        for half_of in range(2):
                            slot = 2 * (b % 2) + half_of
                            act.wait_ge(a_raw[slot], (TURN // 2 * 32) * i + 32 * (o // 2 + b // 2 + 1))
                            nc.scalar.copy(split[:, slot, 0, :], raw[:, slot, :]).then_inc(a_hi, 1)
                        if not (isinstance(g, int) and g == NG - 1):
                            matrices(g + 1, (b + 1) % 2)
                    groups(act, body)

                @block.tensor
                def _(pe):
                    kept = [None]

                    def body(g, b, i):
                        def products(bank, matrices, done):
                            for j in range(GT):
                                slot = 2 * (b % 2) + j // 2
                                for which in range(2):
                                    last = nc.tensor.matmul(
                                        bank[:, :], matrices[:, j, :],
                                        split[:, slot, which, (j % 2) * C:(j % 2 + 1) * C],
                                        start=(j == 0 and which == 0), stop=(j == GT - 1 and which == 1))
                            last.then_inc(done, 1)
                        xs = kept[0] if b else extras_before(pe, g)
                        kept[0] = xe = extras_before(pe, g + 1)
                        with pe.If(xs < xe):
                            with pe.Fori(xs, xe) as n:
                                pe.wait_ge(a_lo, 2 * g + (2 * o + 2))
                                pe.wait_ge(a_hotx, n + 1)
                                products(bankx, hotx, a_px)
                        pe.wait_ge(a_lo, 2 * g + (2 * o + 2))
                        pe.wait_ge(a_hot, g + (o + 1))
                        need(pe, a_acc, g + (o - 1))
                        products(psum[b % 2], hot[:, b % 2, :, :], a_used)
                    groups(pe, body)

                @block.vector
                def _(v):
                    v.sem_inc(a_xacc, 1)

                    def add_main(g, b, w):
                        v.wait_ge(a_used, g + (o + 1))
                        need(v, a_acc, g + o)
                        nc.vector.scalar_tensor_tensor(row(acc, w), psum[b % 2][:, :], rdeg[:, ds(w, 1)],
                                                       row(acc, w), ALU.mult, ALU.add).then_inc(a_acc, 1)

                    def last_window(g):
                        return v.value_load(whi[0:1, ds(g, 1)], min_val=0, max_val=NT - 1)

                    def nearness(g, s, w):
                        need(v, a_dist, g + (o - 1))
                        nc.vector.tensor_scalar(near[:, s, :], dneg[:, ds(g * GT, GT)],
                                                wbase[:, ds(w, 1)], None, ALU.add).then_inc(a_near, 1)

                    kept = [None, last_window(0), None]
                    nearness(0, 0, kept[1])

                    def body(g, b, i):
                        if b == 0 and not isinstance(g, int) or isinstance(g, int) and g == NG - TURN:
                            kept[0], kept[1] = last_window(g - 1), last_window(g)
                        before, w = kept[0], kept[1]
                        after = None
                        if not (isinstance(g, int) and g == NG - 1):
                            after = last_window(g + 1)
                            nearness(g + 1, (b + 1) % 2, after)
                        for half_of in range(2):
                            slot = 2 * (b % 2) + half_of
                            v.wait_ge(a_hi, 2 * g + (2 * o + half_of + 1))
                            nc.vector.tensor_tensor(split[:, slot, 1, :], raw[:, slot, :],
                                                    plain(split[:, slot, 0, :]),
                                                    ALU.subtract).then_inc(a_lo, 1)
                        xs = kept[2] if b else extras_before(v, g)
                        xe = extras_before(v, g + 1)
                        with v.If(xs < xe):
                            with v.Fori(xs, xe) as n:
                                wx = nc.s_assert_within(n - xe + w, 0, NT - 1,
                                                        skip_runtime_bounds_check_because="a visit per window")
                                v.wait_ge(a_xacc, n + 1)
                                nc.vector.tensor_scalar(nearx[:, :], dneg[:, ds(g * GT, GT)],
                                                        wbase[:, ds(wx, 1)], -1.0, ALU.add,
                                                        ALU.mult).then_inc(a_nearx, 1)
                                v.wait_ge(a_nearx, n + 1)
                                nc.vector.tensor_tensor(hotx[:, :, :],
                                                        iota[:, :].unsqueeze(1).to_broadcast([P, GT, P]),
                                                        nearx[:, :].unsqueeze(2).to_broadcast([P, GT, P]),
                                                        ALU.is_equal).then_inc(a_hotx, 1)
                                v.wait_ge(a_px, n + 1)
                                need(v, a_acc, g + (o - 1))
                                nc.vector.scalar_tensor_tensor(row(acc, wx), bankx[:, :], rdeg[:, ds(wx, 1)],
                                                               row(acc, wx), ALU.mult,
                                                               ALU.add).then_inc(a_xacc, 1)
                        if not isinstance(g, int) or g:
                            v.wait_ge(a_xacc, xe + 1)
                            add_main(g - 1, (b - 1) % TURN, before)
                        kept[:] = [w, after, xe]
                    groups(v, body)
                    add_main(NG - 1, TURN - 1, last_window(NG - 1))

        def dense(l):
            load_weights([(w512[l], ws_r), (w512[WN + l], wn_r)], 2 + 2 * l)
            e_b, e_h, e_hi, e_lo, e_s, e_g, e_pT, e_pg, e_ps = (
                sem(f"e{l}_" + n) for n in "b h hi lo s g pT pg ps".split())
            e_gst = [sem(f"e{l}_gst{b}") for b in range(2)]
            with nc.Block() as block:
                @block.sync
                def _(sp):
                    sp.dma_start(bias[:, :], bs[l].partition_broadcast(P)).then_inc(e_b, 16)

                    def store(t, b, k):
                        sp.wait_ge(e_g, t + 1)
                        sp.dma_start(g_tab[l % 2][ds(t * P, P), :], gout[b][:, :]).then_inc(e_gst[b], 16)
                    row_tiles(sp, store)
                    for b in range(2):
                        sp.wait_ge(e_gst[b], 16 * turns(b))

                @block.scalar
                def _(act):
                    def keep_transposed(t, b):
                        act.wait_ge(e_pT, t + 1)
                        need(act, e_ps, t - 1)
                        nc.scalar.copy(hT[b][:, 0, :], psum[b][:, :]).then_inc(e_hi, 1)
                    keep_transposed(0, 0)

                    def body(t, b, k):
                        if not (isinstance(t, int) and t == LAST):
                            keep_transposed(t + 1, 1 - b)
                        act.wait_ge(e_pg, t + 1)
                        need(act, e_gst[b], 16 * k)
                        nc.scalar.copy(gout[b][:, :], psum[2 + b][:, :]).then_inc(e_g, 1)
                    row_tiles(act, body)

                @block.vector
                def _(v):
                    def leaky(t, b):
                        need(v, e_pT, t - 1)
                        nc.vector.scalar_tensor_tensor(h[b][:, :], row(acc, t), SLOPE, row(acc, t),
                                                       ALU.mult, ALU.max).then_inc(e_h, 1)

                    def rest_transposed(t, b):
                        v.wait_ge(e_hi, t + 1)
                        nc.vector.tensor_tensor(hT[b][:, 1, :], psum[b][:, :], plain(hT[b][:, 0, :]),
                                                ALU.subtract).then_inc(e_lo, 1)
                    leaky(0, 0)
                    leaky(1, 1)
                    rest_transposed(0, 0)
                    v.wait_ge(e_b, 16)

                    def body(t, b, k):
                        if not (isinstance(t, int) and t == LAST):
                            rest_transposed(t + 1, 1 - b)
                            if not (isinstance(t, int) and t == LAST - 1):
                                leaky(t + 2, b)
                        v.wait_ge(e_ps, t + 1)
                        nc.vector.tensor_tensor(row(acc, t), psum[4 + b][:, :], bias[:, :],
                                                ALU.add).then_inc(e_s, 1)
                    body(0, 0, 0)
                    body(1, 1, 0)
                    with v.Fori(1, NT // 2 - 1) as i:
                        body(2 * i, 0, i)
                        body(2 * i + 1, 1, i)
                    for t in range(LAST - 2, NT):
                        body(t, t % 2, t // 2)

                @block.tensor
                def _(pe):
                    def turn(t, b):
                        pe.wait_ge(e_h, t + 1)
                        need(pe, e_lo, t - 1)
                        for c in range(KB):
                            last = nc.tensor.transpose(part(psum[b], c), part(h[b], c), ident[:, :])
                        last.then_inc(e_pT, 1)
                    turn(0, 0)

                    def body(t, b, k):
                        if not (isinstance(t, int) and t == LAST):
                            turn(t + 1, 1 - b)
                        pe.wait_ge(e_lo, t + 1)
                        need(pe, e_g, t - 1)
                        product(psum[2 + b][:, :], blocks(hT[b]), weight(wn_r)).then_inc(e_pg, 1)
                        need(pe, e_s, t - 1)
                        product(psum[4 + b][:, :], blocks(hT[b]), weight(ws_r)).then_inc(e_ps, 1)
                    row_tiles(pe, body)

        with conv:
            for l in range(LAYERS):
                if l:
                    dense(l)
                aggregate(l)

        last_part = ExitStack()
        kv = sb("kv", [P, KB, C], f32, last_part)
        wg_sb = sb("wg_sb", [P, KB * EXPERTS], f32, last_part)
        wg_r = sb("wg_r", [P, 2, KB * EXPERTS], f32r, last_part)
        bg_sb = sb("bg_sb", [P, EXPERTS], f32, last_part)
        logits = sb("logits", [P, NT, EXPERTS], f32, last_part)
        cnt = sb("cnt", [P, NT, EXPERTS], f32, last_part)
        cmp = sb("cmp", [P, NT, EXPERTS], f32, last_part)
        top = sb("top", [P, NT], f32, last_part)
        tot = sb("tot", [P, NT], f32, last_part)
        x1T = [sb(f"x1T{b}", [P, 2, C], f32r, last_part) for b in range(2)]
        z = sb("z", [P, 2], f32, last_part)
        stat1 = sb("stat1", [P, 6], f32, last_part)
        mv1 = sb("mv1", [P, 2, 2], f32, last_part)
        rs1 = sb("rs1", [P, 2], f32, last_part)
        plan = Plan(farena)
        xin, qin, x1, xn1 = ([plan.take(C) for _ in range(2)] for _ in range(4))
        mixed, h3 = plan.take(C), plan.take(C)
        f_in = [sem(f"f_in{b}") for b in range(2)]
        f_sx = [sem(f"f_sx{b}") for b in range(2)]
        f_sT = [sem(f"f_sT{b}") for b in range(2)]
        (f_w, f_wg, f_po, f_z, f_mix, f_x1, f_bn, f_var, f_pow, f_xn, f_pT, f_hi, f_lo, f_pl, f_l) = (
            sem("f_" + n) for n in "w wg po z mix x1 bn var pow xn pT hi lo pl l".split())

        def staggered(eng, body):
            for t in range(4):
                body(t, t % 2, t // 2)
            with eng.Fori(2, NT // 2) as i:
                body(2 * i, 0, i)
                body(2 * i + 1, 1, i)
            for t in range(LAST, NT + 2):
                body(t, t % 2, t // 2)

        def live(t, lag):
            return not isinstance(t, int) or 0 <= t - lag < NT

        with nc.Block() as block:
            @block.sync
            def _(sp):
                sp.dma_start(wg_sb[:, :].rearrange("p (k e) -> p k e", k=KB),
                             wg.rearrange("(k p) e -> p k e", p=P)).then_inc(f_w, 16)
                sp.dma_start(bg_sb[:, :], bg.partition_broadcast(P)).then_inc(f_w, 16)
                sp.dma_start(kv[:, :, :].rearrange("p k f -> p (k f)"), kv_tab[:, :]).then_inc(f_w, 16)

                def load(t, b, k):
                    need(sp, f_mix, t - 1)
                    sp.dma_start(xin[b][:, :], dram_tile(x_t, t)).then_inc(f_in[b], 16)
                    sp.dma_start(qin[b][:, :], dram_tile(q_tab, t)).then_inc(f_in[b], 16)
                row_tiles(sp, load)
                sp.wait_ge(f_w, 48)

            @block.scalar
            def _(act):
                act.wait_ge(f_w, 48)
                nc.scalar.copy(wg_r[:, 0, :], wg_sb[:, :]).then_inc(f_wg, 1)

                def body(t, b, k):
                    if live(t, 1):
                        o = 1 - b
                        act.wait_ge(f_pT, t)
                        need(act, f_pl, t - 2)
                        need(act, f_sT[o], 16 * (k - o))
                        nc.scalar.copy(x1T[o][:, 0, :], psum[4 + o][:, :]).then_inc(f_hi, 1)
                staggered(act, body)

            @block.gpsimd
            def _(pool):
                def body(t, b, k):
                    if live(t, 0):
                        pool.wait_ge(f_x1, t + 1)
                        pool.sem_inc(s_gate, 1)
                        pool.dma_start(dram_tile(x1_tab, t), x1[b][:, :]).then_inc(f_sx[b], 16)
                        pool.wait_ge(f_var, t + 1)
                        nc.gpsimd.tensor_tensor(rs1[:, b:b + 1], rs1[:, b:b + 1], half[:, 0:1],
                                                ALU.pow).then_inc(f_pow, 1)
                    if live(t, 1):
                        o = 1 - b
                        pool.wait_ge(f_lo, t)
                        pool.sem_inc(s_gate, 1)
                        pool.dma_start(dram_tile(x1T_tab, t - 1),
                                       x1T[o][:, :, :].rearrange("p a f -> p (a f)")).then_inc(f_sT[o], 16)
                staggered(pool, body)
                for b in range(2):
                    pool.wait_ge(f_sx[b], 16 * turns(b))
                    pool.wait_ge(f_sT[b], 16 * turns(b))

            @block.vector
            def _(v):
                v.wait_ge(f_wg, 1)
                nc.vector.tensor_tensor(wg_r[:, 1, :], wg_sb[:, :], plain(wg_r[:, 0, :]),
                                        ALU.subtract).then_inc(f_wg, 1)

                def body(t, b, k):
                    o = 1 - b
                    if live(t, 0):
                        nc.vector.scalar_tensor_tensor(h3[:, :], row(acc, t), SLOPE, row(acc, t), ALU.mult, ALU.max)
                        v.wait_ge(f_po, t + 1)
                        nc.vector.tensor_scalar(z[:, 0:1], psum[2 + b][:, 0:1], MIX_EPS, None,
                                                ALU.add).then_inc(f_z, 1)
                    if live(t, 1):
                        v.wait_ge(f_pow, t)
                        need(v, f_pT, t - 2)
                        nc.vector.tensor_scalar(xn1[o][:, :], x1[o][:, :], mv1[:, o, 0:1], rs1[:, o:o + 1],
                                                ALU.subtract, ALU.mult).then_inc(f_xn, 1)
                    if live(t, 0):
                        v.wait_ge(f_z, 2 * t + 1)
                        nc.vector.reciprocal(z[:, 1:2], z[:, 0:1]).then_inc(f_z, 1)
                    if live(t, 2):
                        v.wait_ge(f_pl, t - 1)
                        nc.vector.tensor_tensor(row(logits, t - 2), psum[6 + b][:, 0:EXPERTS], bg_sb[:, :],
                                                ALU.add).then_inc(f_l, 1)
                    if live(t, 0):
                        v.wait_ge(f_in[b], 32 * k + 32)
                        v.wait_ge(f_z, 2 * t + 2)
                        nc.vector.scalar_tensor_tensor(mixed[:, :], psum[b][:, :], z[:, 1:2], xin[b][:, :],
                                                       ALU.mult, ALU.add).then_inc(f_mix, 1)
                        v.wait_ge(f_mix, t + 1)
                        need(v, f_sx[b], 16 * k)
                        nc.vector.tensor_tensor(x1[b][:, :], mixed[:, :], h3[:, :], ALU.add).then_inc(f_x1, 1)
                        gate(v, f_x1, t + 1)
                        nc.vector.bn_stats(stat1[:, :], x1[b][:, :]).then_inc(f_bn, 1)
                    if live(t, 1):
                        v.wait_ge(f_hi, t)
                        nc.vector.tensor_tensor(x1T[o][:, 1, :], psum[4 + o][:, :], plain(x1T[o][:, 0, :]),
                                                ALU.subtract).then_inc(f_lo, 1)
                    if live(t, 0):
                        gate(v, f_bn, 2 * t + 1)
                        nc.vector.bn_aggr(mv1[:, b, :], stat1[:, :]).then_inc(f_bn, 1)
                        v.wait_ge(f_bn, 2 * t + 2)
                        nc.vector.tensor_scalar(rs1[:, b:b + 1], mv1[:, b, 1:2], LN_EPS, None,
                                                ALU.add).then_inc(f_var, 1)
                staggered(v, body)

            @block.tensor
            def _(pe):
                pe.wait_ge(f_wg, 2)

                def body(t, b, k):
                    o = 1 - b
                    if live(t, 0):
                        pe.wait_ge(f_in[b], 32 * k + 32)
                        need(pe, f_mix, t - 1)
                        for d in range(KB):
                            nc.tensor.matmul(psum[2 + b][:, 0:1], part(qin[b], d), ksum[:, d:d + 1],
                                             start=(d == 0), stop=(d == KB - 1))
                        for d in range(KB):
                            last = nc.tensor.matmul(psum[b][:, :], part(qin[b], d), kv[:, d, :],
                                                    start=(d == 0), stop=(d == KB - 1))
                        last.then_inc(f_po, 1)
                    if live(t, 2):
                        pe.wait_ge(f_lo, t - 1)
                        need(pe, f_l, t - 3)
                        product(psum[6 + b][:, 0:EXPERTS], blocks(x1T[b]),
                                [(wg_r[:, 0, c * EXPERTS:(c + 1) * EXPERTS],
                                  wg_r[:, 1, c * EXPERTS:(c + 1) * EXPERTS]) for c in range(KB)]).then_inc(f_pl, 1)
                    if live(t, 1):
                        pe.wait_ge(f_xn, t)
                        need(pe, f_lo, t - 2)
                        for c in range(KB):
                            last = nc.tensor.transpose(part(psum[4 + o], c), part(xn1[o], c), ident[:, :])
                        last.then_inc(f_pT, 1)
                staggered(pe, body)

        g_v, g_a = sem("g_v"), sem("g_a")

        def over_experts(ap):
            return ap[:, :].unsqueeze(2).to_broadcast([P, NT, EXPERTS])

        with last_part, nc.Block() as block:
            @block.scalar
            def _(act):
                act.wait_ge(g_v, 2)
                nc.scalar.activation(logits[:, :, :], logits[:, :, :], ACT.Exp).then_inc(g_a, 1)

            @block.vector
            def _(v):
                done = [0]

                def step(ins):
                    ins.then_inc(g_v, 1)
                    done[0] += 1
                    v.wait_ge(g_v, done[0])
                step(nc.vector.tensor_reduce(top[:, :], logits[:, :, :], AX.X, ALU.max))
                step(nc.vector.tensor_tensor(logits[:, :, :], logits[:, :, :], over_experts(top), ALU.subtract))
                v.wait_ge(g_a, 1)
                step(nc.vector.tensor_reduce(tot[:, :], logits[:, :, :], AX.X, ALU.add))
                step(nc.vector.reciprocal(tot[:, :], tot[:, :]))
                step(nc.vector.tensor_tensor(logits[:, :, :], logits[:, :, :], over_experts(tot), ALU.mult))
                step(nc.vector.memset(cnt[:, :, :], 0.0))
                for j in range(EXPERTS):
                    pj = logits[:, :, j:j + 1]
                    if j:
                        nc.vector.tensor_tensor(cmp[:, :, 0:j], logits[:, :, 0:j],
                                                pj.to_broadcast([P, NT, j]), ALU.is_lt)
                    n = EXPERTS - 1 - j
                    if n:
                        nc.vector.tensor_tensor(cmp[:, :, j + 1:], logits[:, :, j + 1:],
                                                pj.to_broadcast([P, NT, n]), ALU.is_le)
                    step(nc.vector.memset(cmp[:, :, j:j + 1], 0.0))
                    step(nc.vector.tensor_tensor(cnt[:, :, :], cnt[:, :, :], cmp[:, :, :], ALU.add))
                step(nc.vector.tensor_scalar(cnt[:, :, :], cnt[:, :, :], 1.5, None, ALU.is_lt))
                step(nc.vector.tensor_tensor(comb[:, :, :], logits[:, :, :], cnt[:, :, :], ALU.mult))
        graph.close()

        WIDE = KB * F
        w1_r = sb("w1_r", [P, 2, EXPERTS * WIDE], f32r)
        w2_r = sb("w2_r", [P, 2, EXPERTS * WIDE], f32r)
        xp = [sb(f"xp{b}", [P, 2, 2, C], f32r) for b in range(2)]
        hm = [sb(f"hm{b}", [P, FB * 2 * P]) for b in range(2)]
        hm_r = [sb(f"hm_r{b}", [P, 2, FB * 2 * P], f32r) for b in range(2)]
        xo = [sb(f"xo{b}", [P, 2, C]) for b in range(2)]
        combT = sb("combT", [P, 2, P])
        cpair = sb("cpair", [P, 2, EXPERTS])
        b1_sb = sb("b1_sb", [P, EXPERTS * FB])
        b2_sb = sb("b2_sb", [P, C])
        wstage = sb("wstage", [P, 4, WIDE])
        h_in = [sem(f"h_in{b}") for b in range(2)]
        h_w = [sem(f"h_w{b}") for b in range(4)]
        h_out = [sem(f"h_out{b}") for b in range(2)]
        (h_ld, h_whi, h_wlo, h_pu, h_gelu, h_hi, h_lo, h_pd, h_acc, h_pc, h_c, h_pb, h_cc) = (
            sem("h_" + n) for n in "ld whi wlo pu gelu hi lo pd acc pc c pb cc".split())
        PAIRS = NT // 2
        PER = 2 * (EXPERTS + 1)

        def hidden(ap, tiles):
            return ap.rearrange("p (f n) -> p f n", f=FB)[:, :, 0:tiles * P]

        def pairs(eng, body):
            body(0, 0, 0, 2)
            body(1, 1, 0, 2)
            with eng.Fori(1, PAIRS // 2) as i:
                body(2 * i, 0, i, 2)
                body(2 * i + 1, 1, i, 2)
            body(PAIRS, 0, PAIRS // 2, 1)

        with nc.Block() as block:
            @block.sync
            def _(sp):
                sp.dma_start(b1_sb[:, :], b1[:, :]).then_inc(h_ld, 16)
                sp.dma_start(b2_sb[0:EXPERTS, :], b2[:, :]).then_inc(h_ld, 16)
                for u in range(2 * EXPERTS):
                    e, source = u // 2, (w1, w2)[u % 2]
                    need(sp, h_wlo, u - 3)
                    src_ap = source[e].rearrange("(k p) f -> p k f", p=P)
                    sp.dma_start(wstage[:, u % 4, :].rearrange("p (k f) -> p k f", k=src_ap.shape[1]),
                                 src_ap).then_inc(h_w[u % 4], 16)

            @block.gpsimd
            def _(pool):
                def load(q, b, k, tiles):
                    gate(pool, h_pu, (q - 1) * EXPERTS)
                    gate(pool, h_out[b], 32 * k)
                    for a in range(tiles):
                        pool.dma_start(xp[b][:, :, a, :],
                                       dram_tile(x1T_tab, 2 * q + a).rearrange("p (s f) -> p s f", s=2)
                                       ).then_inc(h_in[b], 16)
                        pool.dma_start(xo[b][:, a, :], dram_tile(x1_tab, 2 * q + a)).then_inc(h_in[b], 16)

                def store(q, b, tiles):
                    pool.wait_ge(h_acc, q * PER + (EXPERTS + 1) * tiles)
                    pool.sem_inc(s_gate, 1)
                    for a in range(tiles):
                        pool.dma_start(dram_tile(out_t, 2 * q + a), xo[b][:, a, :]).then_inc(h_out[b], 16)

                load(0, 0, 0, 2)
                load(1, 1, 0, 2)
                store(0, 0, 2)
                with pool.Fori(1, PAIRS // 2) as i:
                    load(2 * i, 0, i, 2)
                    store(2 * i - 1, 1, 2)
                    load(2 * i + 1, 1, i, 2)
                    store(2 * i, 0, 2)
                load(PAIRS, 0, PAIRS // 2, 1)
                store(PAIRS - 1, 1, 2)
                store(PAIRS, 0, 1)
                pool.wait_ge(h_out[0], 16 * (2 * (PAIRS // 2) + 1))
                pool.wait_ge(h_out[1], 16 * 2 * (PAIRS // 2))

            def expert_weight(u):
                e, to = u // 2, (w1_r, w2_r)[u % 2]
                return [to[:, s, e * WIDE:(e + 1) * WIDE] for s in range(2)]

            @block.scalar
            def _(act):
                for u in range(2 * EXPERTS):
                    act.wait_ge(h_w[u % 4], 16 * (u // 4 + 1))
                    nc.scalar.copy(expert_weight(u)[0], wstage[:, u % 4, :]).then_inc(h_whi, 1)
                act.wait_ge(h_ld, 32)

                def body(q, b, k, tiles):
                    for e in range(EXPERTS):
                        n = q * EXPERTS + e
                        act.wait_ge(h_pu, n + 1)
                        need(act, h_lo, n - 1)
                        for f in range(FB):
                            last = nc.scalar.activation(
                                hm[e % 2][:, f * 2 * P:f * 2 * P + tiles * P],
                                psum[e % 2][:, f * 2 * P:f * 2 * P + tiles * P],
                                ACT.Gelu_apprx_tanh, bias=b1_sb[:, e * FB + f:e * FB + f + 1])
                        last.then_inc(h_gelu, 1)
                        act.wait_ge(h_gelu, n + 1)
                        need(act, h_pd, n - 1)
                        nc.scalar.copy(hidden(hm_r[e % 2][:, 0, :], tiles), hidden(hm[e % 2], tiles)).then_inc(h_hi, 1)
                pairs(act, body)

            @block.vector
            def _(v):
                for u in range(2 * EXPERTS):
                    hi, lo = expert_weight(u)
                    v.wait_ge(h_whi, u + 1)
                    nc.vector.tensor_tensor(lo, wstage[:, u % 4, :], plain(hi), ALU.subtract).then_inc(h_wlo, 1)

                def body(q, b, k, tiles):
                    def rest(e):
                        v.wait_ge(h_hi, q * EXPERTS + e + 1)
                        nc.vector.tensor_tensor(hidden(hm_r[e % 2][:, 1, :], tiles), hidden(hm[e % 2], tiles),
                                                hidden(plain(hm_r[e % 2][:, 0, :]), tiles),
                                                ALU.subtract).then_inc(h_lo, 1)
                    need(v, h_pc, q)
                    nc.vector.tensor_copy(cpair[:, 0:tiles, :], comb[:, ds(2 * q, tiles), :]).then_inc(h_cc, 1)
                    rest(0)
                    v.wait_ge(h_pc, q + 1)
                    need(v, h_pb, 2 * q)
                    nc.vector.tensor_copy(combT[0:EXPERTS, 0:tiles, :],
                                          psum[6][0:EXPERTS, 0:tiles * P].rearrange("p (a n) -> p a n", a=tiles)
                                          ).then_inc(h_c, 1)
                    v.wait_ge(h_in[b], 64 * k + 32 * tiles)
                    for e in range(EXPERTS):
                        if e + 1 < EXPERTS:
                            rest(e + 1)
                        v.wait_ge(h_pd, q * EXPERTS + e + 1)
                        if e:
                            v.wait_ge(h_acc, q * PER + e * tiles)
                        for a in range(tiles):
                            at = xo[b][:, a, :]
                            nc.vector.scalar_tensor_tensor(at, psum[2 + 2 * (e % 2) + a][:, :],
                                                           row(comb, 2 * q + a)[:, e:e + 1], at,
                                                           ALU.mult, ALU.add).then_inc(h_acc, 1)
                    v.wait_ge(h_acc, q * PER + EXPERTS * tiles)
                    for a in range(tiles):
                        v.wait_ge(h_pb, 2 * q + a + 1)
                        at = xo[b][:, a, :]
                        nc.vector.tensor_tensor(at, psum[7][:, :], at, ALU.add).then_inc(h_acc, 1)
                pairs(v, body)

            @block.tensor
            def _(pe):
                def up(q, b, e, tiles):
                    if isinstance(q, int) and q == 0:
                        pe.wait_ge(h_wlo, 2 * e + 1)
                    need(pe, h_gelu, q * EXPERTS + e - 1)
                    for f in range(FB):
                        w = [[w1_r[:, s, e * WIDE + c * F + f * P:e * WIDE + c * F + (f + 1) * P]
                              for s in range(2)] for c in range(KB)]
                        x_ = [[xp[b][:, s, 0:tiles, c * P:(c + 1) * P] for s in range(2)] for c in range(KB)]
                        last = product(psum[e % 2][:, f * 2 * P:f * 2 * P + tiles * P]
                                       .rearrange("p (a n) -> p a n", a=tiles), w, x_)
                    last.then_inc(h_pu, 1)

                def down(q, e, tiles):
                    if isinstance(q, int) and q == 0:
                        pe.wait_ge(h_wlo, 2 * e + 2)
                    pe.wait_ge(h_lo, q * EXPERTS + e + 1)
                    if e >= 2:
                        pe.wait_ge(h_acc, q * PER + (e - 1) * tiles)
                    else:
                        need(pe, h_acc, q * PER)
                    for a in range(tiles):
                        left = [[hm_r[e % 2][:, s, (2 * f + a) * P:(2 * f + a + 1) * P] for s in range(2)]
                                for f in range(FB)]
                        w = [[w2_r[:, s, e * WIDE + f * C:e * WIDE + (f + 1) * C] for s in range(2)]
                             for f in range(FB)]
                        last = product(psum[2 + 2 * (e % 2) + a][:, :], left, w)
                    last.then_inc(h_pd, 1)

                def body(q, b, k, tiles):
                    pe.wait_ge(h_in[b], 64 * k + 32 * tiles)
                    up(q, b, 0, tiles)
                    pe.wait_ge(h_cc, q + 1)
                    for a in range(tiles):
                        last = nc.tensor.transpose(psum[6][0:EXPERTS, a * P:(a + 1) * P], cpair[:, a, :],
                                                   ident[:, :])
                    last.then_inc(h_pc, 1)
                    for e in range(EXPERTS):
                        if e + 1 < EXPERTS:
                            up(q, b, e + 1, tiles)
                        down(q, e, tiles)
                    for a in range(tiles):
                        pe.wait_ge(h_c, q + 1)
                        need(pe, h_acc, q * PER if a == 0 else q * PER + EXPERTS * tiles + 1)
                        last = nc.tensor.matmul(psum[7][:, :], combT[0:EXPERTS, a, :], b2_sb[0:EXPERTS, :],
                                                start=True, stop=True)
                        last.then_inc(h_pb, 1)
                pairs(pe, body)


def kernel(x, src, dst, **w):
    import numpy as np
    import concourse.bacc as bacc
    from concourse.bass_utils import run_bass_kernel_spmd as run

    xp = np.concatenate([x, np.zeros((NPAD - N, C), np.float32)])
    pad = EPAD - E
    wqk = np.asarray(w["L0_mix_W_qk"])
    s = np.concatenate([src, np.zeros(pad, np.int32)])
    d = np.concatenate([dst, np.full(pad, NPAD - 1, np.int32)])
    a = {
        "x": xp,
        "src": s.reshape(HALVES, 2 * GT, P).transpose(0, 2, 1),
        "dst": d.reshape(NE, P).T,
        "dstg": d.reshape(NG // 2, 2, GT * P),
        "w512": np.stack([w[f"L0_gnn_w_self{i}"] for i in range(LAYERS)]
                          + [w[f"L0_gnn_w_neigh{i}"] for i in range(LAYERS)]
                          + [wqk[:C].T, wqk[C:].T]),
        "bs": np.stack([w[f"L0_gnn_b{i}"] for i in range(LAYERS)]),
        "wg": w["L0_ffn_Wg"], "bg": w["L0_ffn_bg"],
        "w1": w["L0_ffn_W1"],
        "b1": np.asarray(w["L0_ffn_b1"]).reshape(EXPERTS * FB, P).T,
        "w2": w["L0_ffn_W2"], "b2": w["L0_ffn_b2"],
    }
    a = {k: np.ascontiguousarray(v) for k, v in a.items()}
    nc = bacc.Bacc("TRN2", target_bir_lowering=False, num_devices=1)
    args = {k: nc.dram_tensor("in_" + k, v.shape, mybir.dt.from_np(v.dtype), kind="ExternalInput").ap()
            for k, v in a.items()}
    out = nc.dram_tensor("out", (NPAD, C), mybir.dt.float32, kind="ExternalOutput").ap()
    build_kernel(nc, out=out, **args)
    r = run(nc, [{"in_" + k: v for k, v in a.items()}], core_ids=[0])
    return r.results[0]["out"][:N]
```
